# Optimizing a Trainium2 kernel written in Bass

```python
import numpy as np
import jax
import jax.numpy as jnp

def _softmax(x, axis=-1):
    return jax.nn.softmax(x, axis=axis)

def _gelu(x):
    return jax.nn.gelu(x, approximate=True)

def _silu(x):
    return jax.nn.silu(x)

def _sigmoid(x):
    return jax.nn.sigmoid(x)

def _layernorm(x, axis=-1, eps=1e-05):
    m = jnp.mean(x, axis=axis, keepdims=True)
    v = jnp.var(x, axis=axis, keepdims=True)
    return (x - m) / jnp.sqrt(v + eps)

def _scatter_add(tgt, idx, src, axis=0):
    return tgt.at[idx].add(src)

def _segment_sum(src, seg, n):
    return jax.ops.segment_sum(src, seg, n)
kernel_name = 'mk_dlrm_tower_d1_rec_r8_e9e02f'

def setup_inputs(seed: int=0):
    np.random.seed(seed)
    _w = jnp.asarray

    def _rec_inputs():
        import jax
        import jax.numpy as jnp
        _tk = jax.random.key(seed)
        dense_ctx = jax.random.normal(jax.random.fold_in(_tk, 190), (2048, 16), jnp.float32)
        ids = jnp.stack([jax.random.randint(jax.random.fold_in(_tk, 200 + f), (2048,), 0, v, jnp.int32) for f, v in enumerate([125000, 12500, 1250, 1250, 125000, 1250, 12500, 1250, 1250, 125000, 12500, 12500, 125000, 12500, 125000, 1000, 1250, 12500, 125000, 1000, 1000, 1250, 1000, 12500, 1000, 1250, 1250, 1250, 12500, 12500, 1000, 1000, 1000, 1250, 12500, 1250, 125000, 125000, 12500])], axis=1)
        tbl_0 = 0.05 * jax.random.normal(jax.random.fold_in(_tk, 500 + 0), (125000, 16), jnp.float32)
        tbl_1 = 0.05 * jax.random.normal(jax.random.fold_in(_tk, 500 + 1), (12500, 16), jnp.float32)
        tbl_2 = 0.05 * jax.random.normal(jax.random.fold_in(_tk, 500 + 2), (1250, 16), jnp.float32)
        tbl_3 = 0.05 * jax.random.normal(jax.random.fold_in(_tk, 500 + 3), (1250, 16), jnp.float32)
        tbl_4 = 0.05 * jax.random.normal(jax.random.fold_in(_tk, 500 + 4), (125000, 16), jnp.float32)
        tbl_5 = 0.05 * jax.random.normal(jax.random.fold_in(_tk, 500 + 5), (1250, 16), jnp.float32)
        tbl_6 = 0.05 * jax.random.normal(jax.random.fold_in(_tk, 500 + 6), (12500, 16), jnp.float32)
        tbl_7 = 0.05 * jax.random.normal(jax.random.fold_in(_tk, 500 + 7), (1250, 16), jnp.float32)
        tbl_8 = 0.05 * jax.random.normal(jax.random.fold_in(_tk, 500 + 8), (1250, 16), jnp.float32)
        tbl_9 = 0.05 * jax.random.normal(jax.random.fold_in(_tk, 500 + 9), (125000, 16), jnp.float32)
        tbl_10 = 0.05 * jax.random.normal(jax.random.fold_in(_tk, 500 + 10), (12500, 16), jnp.float32)
        tbl_11 = 0.05 * jax.random.normal(jax.random.fold_in(_tk, 500 + 11), (12500, 16), jnp.float32)
        tbl_12 = 0.05 * jax.random.normal(jax.random.fold_in(_tk, 500 + 12), (125000, 16), jnp.float32)
        tbl_13 = 0.05 * jax.random.normal(jax.random.fold_in(_tk, 500 + 13), (12500, 16), jnp.float32)
        tbl_14 = 0.05 * jax.random.normal(jax.random.fold_in(_tk, 500 + 14), (125000, 16), jnp.float32)
        tbl_15 = 0.05 * jax.random.normal(jax.random.fold_in(_tk, 500 + 15), (1000, 16), jnp.float32)
        tbl_16 = 0.05 * jax.random.normal(jax.random.fold_in(_tk, 500 + 16), (1250, 16), jnp.float32)
        tbl_17 = 0.05 * jax.random.normal(jax.random.fold_in(_tk, 500 + 17), (12500, 16), jnp.float32)
        tbl_18 = 0.05 * jax.random.normal(jax.random.fold_in(_tk, 500 + 18), (125000, 16), jnp.float32)
        tbl_19 = 0.05 * jax.random.normal(jax.random.fold_in(_tk, 500 + 19), (1000, 16), jnp.float32)
        tbl_20 = 0.05 * jax.random.normal(jax.random.fold_in(_tk, 500 + 20), (1000, 16), jnp.float32)
        tbl_21 = 0.05 * jax.random.normal(jax.random.fold_in(_tk, 500 + 21), (1250, 16), jnp.float32)
        tbl_22 = 0.05 * jax.random.normal(jax.random.fold_in(_tk, 500 + 22), (1000, 16), jnp.float32)
        tbl_23 = 0.05 * jax.random.normal(jax.random.fold_in(_tk, 500 + 23), (12500, 16), jnp.float32)
        tbl_24 = 0.05 * jax.random.normal(jax.random.fold_in(_tk, 500 + 24), (1000, 16), jnp.float32)
        tbl_25 = 0.05 * jax.random.normal(jax.random.fold_in(_tk, 500 + 25), (1250, 16), jnp.float32)
        tbl_26 = 0.05 * jax.random.normal(jax.random.fold_in(_tk, 500 + 26), (1250, 16), jnp.float32)
        tbl_27 = 0.05 * jax.random.normal(jax.random.fold_in(_tk, 500 + 27), (1250, 16), jnp.float32)
        tbl_28 = 0.05 * jax.random.normal(jax.random.fold_in(_tk, 500 + 28), (12500, 16), jnp.float32)
        tbl_29 = 0.05 * jax.random.normal(jax.random.fold_in(_tk, 500 + 29), (12500, 16), jnp.float32)
        tbl_30 = 0.05 * jax.random.normal(jax.random.fold_in(_tk, 500 + 30), (1000, 16), jnp.float32)
        tbl_31 = 0.05 * jax.random.normal(jax.random.fold_in(_tk, 500 + 31), (1000, 16), jnp.float32)
        tbl_32 = 0.05 * jax.random.normal(jax.random.fold_in(_tk, 500 + 32), (1000, 16), jnp.float32)
        tbl_33 = 0.05 * jax.random.normal(jax.random.fold_in(_tk, 500 + 33), (1250, 16), jnp.float32)
        tbl_34 = 0.05 * jax.random.normal(jax.random.fold_in(_tk, 500 + 34), (12500, 16), jnp.float32)
        tbl_35 = 0.05 * jax.random.normal(jax.random.fold_in(_tk, 500 + 35), (1250, 16), jnp.float32)
        tbl_36 = 0.05 * jax.random.normal(jax.random.fold_in(_tk, 500 + 36), (125000, 16), jnp.float32)
        tbl_37 = 0.05 * jax.random.normal(jax.random.fold_in(_tk, 500 + 37), (125000, 16), jnp.float32)
        tbl_38 = 0.05 * jax.random.normal(jax.random.fold_in(_tk, 500 + 38), (12500, 16), jnp.float32)
        _rk = jax.random.fold_in(_tk, 7)
        W_top1 = 0.0606339 * jax.random.normal(jax.random.fold_in(_tk, 801), (272, 512), jnp.float32)
        W_top2 = 0.0441942 * jax.random.normal(jax.random.fold_in(_tk, 802), (512, 256), jnp.float32)
        W_top3 = 0.0625 * jax.random.normal(jax.random.fold_in(_tk, 803), (256, 1), jnp.float32)
        b_top1 = jnp.zeros((512,), jnp.float32)
        b_top2 = jnp.zeros((256,), jnp.float32)
        return (dense_ctx, ids, tbl_0, tbl_1, tbl_2, tbl_3, tbl_4, tbl_5, tbl_6, tbl_7, tbl_8, tbl_9, tbl_10, tbl_11, tbl_12, tbl_13, tbl_14, tbl_15, tbl_16, tbl_17, tbl_18, tbl_19, tbl_20, tbl_21, tbl_22, tbl_23, tbl_24, tbl_25, tbl_26, tbl_27, tbl_28, tbl_29, tbl_30, tbl_31, tbl_32, tbl_33, tbl_34, tbl_35, tbl_36, tbl_37, tbl_38, W_top1, b_top1, W_top2, b_top2, W_top3)
    dense_ctx, ids, tbl_0, tbl_1, tbl_2, tbl_3, tbl_4, tbl_5, tbl_6, tbl_7, tbl_8, tbl_9, tbl_10, tbl_11, tbl_12, tbl_13, tbl_14, tbl_15, tbl_16, tbl_17, tbl_18, tbl_19, tbl_20, tbl_21, tbl_22, tbl_23, tbl_24, tbl_25, tbl_26, tbl_27, tbl_28, tbl_29, tbl_30, tbl_31, tbl_32, tbl_33, tbl_34, tbl_35, tbl_36, tbl_37, tbl_38, W_top1, b_top1, W_top2, b_top2, W_top3 = _rec_inputs()

    def _L0_rec_setup():
        import jax, jax.numpy as jnp
        import numpy as np
        NUM_FIELD = 39
        CIN_SIZE = [128, 128]
        EMBED_DIM = 16
        BATCH = 256
        key = jax.random.key(seed)
        k1, k2, k3 = jax.random.split(key, 3)
        x_emb = jax.random.normal(k1, (BATCH, NUM_FIELD, EMBED_DIM), dtype=jnp.float32)
        W0 = jax.random.normal(k2, (CIN_SIZE[0], NUM_FIELD * NUM_FIELD), dtype=jnp.float32) * 0.02
        W1 = jax.random.normal(k3, (CIN_SIZE[1], CIN_SIZE[0] * NUM_FIELD), dtype=jnp.float32) * 0.02
        return {'x_emb': x_emb, 'W0': W0, 'W1': W1}
    _L0_rec_all = _L0_rec_setup()
    _L0_rec_in = {k: v for k, v in _L0_rec_all.items() if k in ('W0', 'W1')}
    del _L0_rec_all
    return {'dense_ctx': dense_ctx, 'ids': ids, 'tbl_0': tbl_0, 'tbl_1': tbl_1, 'tbl_2': tbl_2, 'tbl_3': tbl_3, 'tbl_4': tbl_4, 'tbl_5': tbl_5, 'tbl_6': tbl_6, 'tbl_7': tbl_7, 'tbl_8': tbl_8, 'tbl_9': tbl_9, 'tbl_10': tbl_10, 'tbl_11': tbl_11, 'tbl_12': tbl_12, 'tbl_13': tbl_13, 'tbl_14': tbl_14, 'tbl_15': tbl_15, 'tbl_16': tbl_16, 'tbl_17': tbl_17, 'tbl_18': tbl_18, 'tbl_19': tbl_19, 'tbl_20': tbl_20, 'tbl_21': tbl_21, 'tbl_22': tbl_22, 'tbl_23': tbl_23, 'tbl_24': tbl_24, 'tbl_25': tbl_25, 'tbl_26': tbl_26, 'tbl_27': tbl_27, 'tbl_28': tbl_28, 'tbl_29': tbl_29, 'tbl_30': tbl_30, 'tbl_31': tbl_31, 'tbl_32': tbl_32, 'tbl_33': tbl_33, 'tbl_34': tbl_34, 'tbl_35': tbl_35, 'tbl_36': tbl_36, 'tbl_37': tbl_37, 'tbl_38': tbl_38, 'W_top1': W_top1, 'b_top1': b_top1, 'W_top2': W_top2, 'b_top2': b_top2, 'W_top3': W_top3, 'L0_rec_W0': _L0_rec_in['W0'], 'L0_rec_W1': _L0_rec_in['W1']}

def reference(dense_ctx, ids, tbl_0, tbl_1, tbl_2, tbl_3, tbl_4, tbl_5, tbl_6, tbl_7, tbl_8, tbl_9, tbl_10, tbl_11, tbl_12, tbl_13, tbl_14, tbl_15, tbl_16, tbl_17, tbl_18, tbl_19, tbl_20, tbl_21, tbl_22, tbl_23, tbl_24, tbl_25, tbl_26, tbl_27, tbl_28, tbl_29, tbl_30, tbl_31, tbl_32, tbl_33, tbl_34, tbl_35, tbl_36, tbl_37, tbl_38, W_top1, b_top1, W_top2, b_top2, W_top3, L0_rec_W0, L0_rec_W1):
    import jax
    import jax.numpy as jnp

    def _L0_rec_ref(x_emb, W0, W1):
        import jax, jax.numpy as jnp
        import numpy as np
        NUM_FIELD = 39
        CIN_SIZE = [128, 128]
        EMBED_DIM = 16
        BATCH = 256
        B, F, D = x_emb.shape
        x = x_emb
        outs = []
        for W in (W0, W1):
            last = x.shape[1]
            inter = (x[:, :, None, :] * x_emb[:, None, :, :]).reshape(B, last * F, D)
            x = jnp.einsum('bid,hi->bhd', inter, W)
            outs.append(x.sum(axis=-1))
        return jnp.concatenate(outs, axis=-1)
    e = jnp.stack([tbl_0[ids[:, 0]], tbl_1[ids[:, 1]], tbl_2[ids[:, 2]], tbl_3[ids[:, 3]], tbl_4[ids[:, 4]], tbl_5[ids[:, 5]], tbl_6[ids[:, 6]], tbl_7[ids[:, 7]], tbl_8[ids[:, 8]], tbl_9[ids[:, 9]], tbl_10[ids[:, 10]], tbl_11[ids[:, 11]], tbl_12[ids[:, 12]], tbl_13[ids[:, 13]], tbl_14[ids[:, 14]], tbl_15[ids[:, 15]], tbl_16[ids[:, 16]], tbl_17[ids[:, 17]], tbl_18[ids[:, 18]], tbl_19[ids[:, 19]], tbl_20[ids[:, 20]], tbl_21[ids[:, 21]], tbl_22[ids[:, 22]], tbl_23[ids[:, 23]], tbl_24[ids[:, 24]], tbl_25[ids[:, 25]], tbl_26[ids[:, 26]], tbl_27[ids[:, 27]], tbl_28[ids[:, 28]], tbl_29[ids[:, 29]], tbl_30[ids[:, 30]], tbl_31[ids[:, 31]], tbl_32[ids[:, 32]], tbl_33[ids[:, 33]], tbl_34[ids[:, 34]], tbl_35[ids[:, 35]], tbl_36[ids[:, 36]], tbl_37[ids[:, 37]], tbl_38[ids[:, 38]]], axis=1)
    z = _L0_rec_ref(e, L0_rec_W0, L0_rec_W1)
    z = z.reshape(z.shape[0], -1)
    h = jnp.concatenate([z, dense_ctx], axis=1)
    h = jnp.maximum(h @ W_top1 + b_top1, 0.0)
    h = jnp.maximum(h @ W_top2 + b_top2, 0.0)
    y = h @ W_top3
    return y

_drawn_inputs = setup_inputs


def setup_inputs(seed=0):
    import zlib

    import numpy as np

    out = dict(_drawn_inputs(seed))
    spreads = {'b_top1': (0.0, 0.1), 'b_top2': (0.0, 0.1)}
    factors = {'tbl_0': 8.0,
     'tbl_1': 8.0,
     'tbl_2': 8.0,
     'tbl_3': 8.0,
     'tbl_4': 8.0,
     'tbl_5': 8.0,
     'tbl_6': 8.0,
     'tbl_7': 8.0,
     'tbl_8': 8.0,
     'tbl_9': 8.0,
     'tbl_10': 8.0,
     'tbl_11': 8.0,
     'tbl_12': 8.0,
     'tbl_13': 8.0,
     'tbl_14': 8.0,
     'tbl_15': 8.0,
     'tbl_16': 8.0,
     'tbl_17': 8.0,
     'tbl_18': 8.0,
     'tbl_19': 8.0,
     'tbl_20': 8.0,
     'tbl_21': 8.0,
     'tbl_22': 8.0,
     'tbl_23': 8.0,
     'tbl_24': 8.0,
     'tbl_25': 8.0,
     'tbl_26': 8.0,
     'tbl_27': 8.0,
     'tbl_28': 8.0,
     'tbl_29': 8.0,
     'tbl_30': 8.0,
     'tbl_31': 8.0,
     'tbl_32': 8.0,
     'tbl_33': 8.0,
     'tbl_34': 8.0,
     'tbl_35': 8.0,
     'tbl_36': 8.0,
     'tbl_37': 8.0,
     'tbl_38': 8.0,
     'L0_rec_W1': 8.0}
    for name, (base, spread) in spreads.items():
        noise = np.random.default_rng([zlib.crc32(name.encode()), seed]).standard_normal(out[name].shape)
        drawn = base * np.exp(spread * noise) if base else spread * noise
        out[name] = jnp.asarray(drawn.astype(out[name].dtype))
    for name, factor in factors.items():
        out[name] = (out[name] * factor).astype(out[name].dtype)
    return out
```

```python
import concourse.bass as bass
from concourse import mybir
from contextlib import ExitStack

FIELDS, DIM, HID = 39, 16, 128
BATCH = 2048
TILE = 128
TILES = BATCH // TILE
CHUNKS = 4
COLS = TILE * DIM // CHUNKS
NT = COLS // 128
PARTS = 3 * FIELDS
PAIRS = FIELDS * (FIELDS + 1) // 2
FULL = PAIRS // 128
REST = PAIRS - 128 * FULL
KT = FULL + 1
REST_ROWS = 96
STEPS = CHUNKS * KT
AHEAD = 3
GJ = FIELDS + 1
QUAD = 4
H1, H2 = 512, 256


def cin_tower_kernel(nc, ids, tables, w0_pair, w0_swap, w0_rows, w1t, top1, b1, top2, b2, top3, dense_t,
                     c_sel, c_sum3, c_ident, c_diag, out):
    fp32, bf16, f32r, i32 = mybir.dt.float32, mybir.dt.bfloat16, mybir.dt.float32r, mybir.dt.int32
    ALU = mybir.AluOpType
    ACT = mybir.ActivationFunctionType
    AX = mybir.AxisListType

    ctx = ExitStack()
    with ctx:
        def sb(name, shape, dt, where=ctx):
            return where.enter_context(nc.sbuf_tensor(name, shape, dt))

        def pb(name, shape, dt=fp32):
            return ctx.enter_context(nc.psum_tensor(name, shape, dt))

        def sem(name):
            return ctx.enter_context(nc.semaphore(name))

        sel = sb("sel", [PARTS, KT, 128], bf16)
        sum3 = sb("sum3", [PARTS, GJ], bf16)
        ident = sb("ident", [128, 128], fp32)
        ident_b = sb("ident_b", [128, 128], bf16)
        v_hi = sb("v_hi", [128, KT, HID], f32r)
        v_lo = sb("v_lo", [128, KT, HID], f32r)
        w1 = sb("w1", [128, FIELDS, 2 * HID], f32r)
        ids_sb = [sb(f"ids{s}", [128, FIELDS], i32) for s in range(2)]
        emb = [sb(f"emb{s}", [128, FIELDS, DIM], fp32) for s in range(2)]
        resid = sb("resid", [128, FIELDS, DIM], fp32)
        parts = sb("parts", [128, DIM, 3, FIELDS], bf16)
        emb_t = [sb(f"emb_t{s}", [PARTS, TILE, DIM], bf16) for s in range(2)]
        sq = [sb(f"sq{s}", [128, COLS], fp32) for s in range(2)]
        sq_hi = [sb(f"sq_hi{s}", [128, COLS], f32r) for s in range(4)]
        sq_lo = [sb(f"sq_lo{s}", [128, COLS], f32r) for s in range(4)]
        x1 = [sb(f"x1{s}", [128, COLS], fp32) for s in range(2)]
        xt_hi = sb("xt_hi", [128, NT, HID], f32r)
        xt_lo = sb("xt_lo", [128, NT, HID], f32r)
        en = [sb(f"en{s}", [128, 2, NT, GJ], f32r) for s in range(2)]
        bd = [sb(f"bd{s}", [128, 2, NT, QUAD, GJ], f32r) for s in range(2)]
        z1_all = sb("z1_all", [128, BATCH], fp32)
        z2_all = sb("z2_all", [128, TILES, HID], fp32)
        z2_part = sb("z2_part", [128, HID], fp32)
        with ExitStack() as room:
            g_hi = [sb(f"g_hi{s}", [128, GJ, TILE], f32r, room) for s in range(2)]
            g_lo = [sb(f"g_lo{s}", [128, GJ, TILE], f32r, room) for s in range(2)]
        with ExitStack() as room:
            r_w1 = sb("r_w1", [128, FIELDS, HID], fp32, room)
            r_pair = sb("r_pair", [128, KT, HID], fp32, room)
            r_swap = sb("r_swap", [128, KT, HID], fp32, room)
            r_rows = sb("r_rows", [FIELDS, HID, 2 * FIELDS], fp32, room)
            r_sel = sb("r_sel", [PARTS, KT, 128], fp32, room)
            r_sum3 = sb("r_sum3", [PARTS, GJ], fp32, room)
            r_diag = sb("r_diag", [128, 2, QUAD, GJ], fp32, room)
            r_tot = sb("r_tot", [FIELDS, HID], fp32, room)
            r_half = sb("r_half", [FIELDS, HID], fp32, room)
        with ExitStack() as room:
            t_top1 = sb("t_top1", [128, 2, H1], fp32, room)
            t_top1d = sb("t_top1d", [DIM, H1], fp32, room)
            t_top2 = sb("t_top2", [128, H1 // 128, H2], fp32, room)
            t_top3 = sb("t_top3", [128, H2 // 128], fp32, room)
            t_b1 = sb("t_b1", [128, H1 // 128], fp32, room)
            t_b2 = sb("t_b2", [128, H2 // 128], fp32, room)
            t_dense = sb("t_dense", [DIM, BATCH], fp32, room)
            z2_t = sb("z2_t", [128, 512], fp32, room)
            h1_sb = sb("h1_sb", [128, H1 // 128, 512], fp32, room)
            h2_sb = sb("h2_sb", [128, H2 // 128, 512], fp32, room)
            y_sb = sb("y_sb", [1, BATCH], fp32, room)

        p_sum = [pb(f"p_sum{s}", [128, COLS]) for s in range(2)]
        p_x1 = pb("p_x1", [128, COLS])
        p_xt = pb("p_xt", [128, NT, HID])
        p_misc = pb("p_misc", [128, 512])
        p_misc_b = p_misc[:, :].bitcast(bf16)
        p_g = pb("p_g", [128, 2, 512])
        p_z2 = pb("p_z2", [128, 512])

        gather_begun = sem("gather_begun")
        consts_in, top_in, y_out = sem("consts_in"), sem("top_in"), sem("y_out")
        ids_in = [sem(f"ids_in{s}") for s in range(2)]
        emb_in = [sem(f"emb_in{s}") for s in range(2)]
        bd_in = [sem(f"bd_in{s}") for s in range(2)]
        prep = sem("prep")
        parts_done = sem("parts_done")
        et_mm, et_out = sem("et_mm"), sem("et_out")
        en_mm, en_h, en_l = sem("en_mm"), sem("en_h"), sem("en_l")
        sum_mm, sq_done, hi_done, lo_done, prod_mm = (sem(n) for n in ("sum_mm", "sq_done", "hi_done", "lo_done", "prod_mm"))
        x1_out, xt_mm, xt_h, xt_l = sem("x1_out"), sem("xt_mm"), sem("xt_h"), sem("xt_l")
        g_mm, g_h, g_l = sem("g_mm"), sem("g_h"), sem("g_l")
        z2_mm, z2_a, z2_b, z1_done = sem("z2_mm"), sem("z2_a"), sem("z2_b"), sem("z1_done")
        tail_pe, tail_act = sem("tail_pe"), sem("tail_act")

        PREPARED = 14

        def g_view(buf, c, h):
            return buf[:, :, 32 * c:32 * c + 32].rearrange("p j (r h m) -> p r h m j", r=2, h=2)[:, :, h, :, :]

        def g_bank_view():
            return p_g[:, :, 0:2 * QUAD * GJ].rearrange("p r (m j) -> p r m j", j=GJ)

        def cnt(t, per_tile, more=0):
            reg, at = t
            if reg is None:
                return per_tile * at + more
            return reg * (2 * per_tile) + (per_tile * at + more)

        def ge(eng, s, value):
            if not isinstance(value, int) or value > 0:
                eng.wait_ge(s, value)

        def over_tiles(eng, tile):
            tile((None, 0), 0, first=True, last=False)
            with eng.Fori(0, (TILES - 2) // 2) as i:
                tile((i, 1), 1, first=False, last=False)
                tile((i, 2), 0, first=False, last=False)
            tile((None, TILES - 1), 1, first=False, last=True)

        ET_AT = (2 * KT + 5, 3 * KT + 2)
        PARTS_AT = (2 * KT, 2 * KT + 1, 2 * KT + 2, 2 * KT + 3)
        Z2_FROM = KT
        Z1_AT = KT + 3
        XT_AT, G_AT = 2, (4, 6)

        block = ctx.enter_context(nc.Block())

        @block.sync
        def _(sp):
            def load_ids(t, s, after=None):
                reg, at = t
                row = at * TILE if reg is None else sp.snap(reg * (2 * TILE) + at * TILE)
                if after is not None:
                    sp.wait_ge(emb_in[s], after)
                sp.dma_start(ids_sb[s][:, :], ids[bass.ds(row, TILE), :]).then_inc(ids_in[s], 16)

            load_ids((None, 0), 0)
            load_ids((None, 1), 1)
            for dst, src in ((r_sel[:, :, :], c_sel), (r_sum3[:, :], c_sum3), (ident[:, :], c_ident),
                             (r_diag[:, :, :, :], c_diag), (r_rows[:, :, :], w0_rows),
                             (r_pair[:, :, :], w0_pair), (r_swap[:, :, :], w0_swap), (r_w1[:, :, :], w1t)):
                sp.dma_start(dst, src).then_inc(consts_in, 16)

            def tile(t, s, more):
                for c in range(CHUNKS):
                    cs = c % 2
                    if c == 1 and more:
                        load_ids((t[0], t[1] + 2), s, emb_count(t, s))
                    sp.wait_ge(en_l, cnt(t, CHUNKS, c + 1))
                    for b in range(8):
                        rows = slice(b * DIM, (b + 1) * DIM)
                        sp.dma_start(bd[cs][rows, :, :, b % QUAD, 0:FIELDS].bitcast(fp32),
                                     en[cs][rows, :, :, 0:FIELDS].bitcast(fp32)).then_inc(bd_in[cs], 16)

            def emb_count(t, s):
                reg, at = t
                if reg is None:
                    return 16 * FIELDS * (at // 2 + 1)
                return reg * (16 * FIELDS) + 16 * FIELDS * (at // 2 + 1)

            sp.wait_ge(prep, PREPARED)
            tile((None, 0), 0, more=True)
            with sp.Fori(0, (TILES - 4) // 2) as i:
                tile((i, 1), 1, more=True)
                tile((i, 2), 0, more=True)
            tile((None, TILES - 3), 1, more=True)
            tile((None, TILES - 2), 0, more=False)
            tile((None, TILES - 1), 1, more=False)

            sp.wait_ge(z2_mm, TILES - 1)
            sp.wait_ge(z1_done, TILES - 1)
            for dst, src in ((t_top1[:, :, :], top1[0:2 * HID, :].rearrange("(k p) n -> p k n", p=128)),
                             (t_top1d[:, :], top1[2 * HID:2 * HID + DIM, :]),
                             (t_top2[:, :, :], top2.rearrange("(k p) n -> p k n", p=128)),
                             (t_top3[:, :], top3), (t_b1[:, :], b1), (t_b2[:, :], b2), (t_dense[:, :], dense_t)):
                sp.dma_start(dst, src).then_inc(top_in, 16)
            sp.wait_ge(tail_act, 4 * 8)
            sp.dma_start(out, y_sb[:, :]).then_inc(y_out, 16)
            sp.wait_ge(y_out, 16)

        @block.gpsimd
        def _(pool):
            def gather(t, s, first):
                if first:
                    pool.wait_ge(ids_in[s], 16)
                else:
                    pool.wait_ge(ids_in[s], t * 16 + 16)
                    pool.wait_ge(parts_done, t * 8 + (4 * s - 6))
                    pool.sem_inc(gather_begun, 1)
                for f in range(FIELDS):
                    nc.gpsimd.indirect_dma_start(
                        out=emb[s][:, f, :], out_offset=None, in_=tables[f],
                        in_offset=bass.IndirectOffsetOnAxis(ap=ids_sb[s][:, f:f + 1], axis=0)).then_inc(emb_in[s], 16)

            gather(0, 0, True)
            gather(0, 1, True)
            with pool.Fori(1, TILES // 2) as pair:
                gather(pair, 0, False)
                gather(pair, 1, False)

        @block.tensor
        def _(pe):
            def embeddings_t(t, r, s):
                pe.wait_ge(parts_done, cnt(t, 4, 4))
                for d in range(8):
                    last = nc.tensor.transpose(p_misc_b[0:PARTS, d * 128:(d + 1) * 128],
                                               parts[:, 8 * r + d, :, :].rearrange("p a f -> p (a f)"), ident_b[:, :])
                last.then_inc(et_mm, 1)

            def pair_sums(t, s, step):
                c, k = divmod(step, KT)
                ge(pe, sq_done, cnt(t, STEPS, step - 1))
                nc.tensor.matmul(p_sum[step % 2][:, :], sel[:, k, :],
                                 emb_t[s][:, c * 32:(c + 1) * 32, :].rearrange("p b d -> p (b d)"),
                                 start=True, stop=True).then_inc(sum_mm, 1)

            def products(t, step):
                c, k = divmod(step, KT)
                r = step % 4
                if k == 0:
                    ge(pe, x1_out, cnt(t, CHUNKS, c))
                pe.wait_ge(lo_done, cnt(t, STEPS, step + 1))
                if k < FULL:
                    nc.tensor.matmul(p_x1[:, :], v_hi[:, k, :], sq_hi[r][:, :], start=(k == 0), stop=False)
                    nc.tensor.matmul(p_x1[:, :], v_lo[:, k, :], sq_hi[r][:, :], start=False, stop=False)
                    nc.tensor.matmul(p_x1[:, :], v_hi[:, k, :], sq_lo[r][:, :], start=False, stop=False).then_inc(prod_mm, 1)
                else:
                    nc.tensor.matmul(p_x1[:, :], v_hi[0:REST_ROWS, k, :], sq_hi[r][0:REST_ROWS, :], start=False,
                                     stop=True).then_inc(prod_mm, 1)

            def embeddings_n(t, s, c, last):
                ge(pe, en_l, cnt(t, CHUNKS, c))
                if c == 0:
                    pe.wait_ge(et_out, cnt(t, 2, 2))
                if c == 3 and not last:
                    pe.wait_ge(et_out, cnt(t, 2, 3))
                for n in range(NT):
                    b = c * 32 + n * 8
                    mm = nc.tensor.matmul(p_misc[:, n * GJ:(n + 1) * GJ],
                                            emb_t[s][:, b:b + 8, :].rearrange("p b d -> p (b d)"), sum3[:, :],
                                            start=True, stop=True)
                mm.then_inc(en_mm, 1)

            def x1_transposed(q):
                pe.wait_ge(x1_out, q)
                ge(pe, xt_l, q - 1)
                for n in range(NT):
                    last = nc.tensor.transpose(p_xt[:, n, :], x1_prev[0][:, n * 128:(n + 1) * 128], ident[:, :])
                last.then_inc(xt_mm, 1)

            x1_prev = [None]

            def g_half(q, cs, h):
                if h == 0:
                    pe.wait_ge(xt_l, q)
                    pe.wait_ge(bd_in[cs], bd_count[0])
                ge(pe, g_l, q * 2 - 2 + h)
                for n in (2 * h, 2 * h + 1):
                    for r in range(2):
                        rows = slice(64 * r, 64 * r + 64)
                        o = p_g[:, r, (n % 2) * QUAD * GJ:(n % 2 + 1) * QUAD * GJ]
                        b_hi = bd[cs][rows, 0, n, :, :].rearrange("p b j -> p (b j)")
                        b_lo = bd[cs][rows, 1, n, :, :].rearrange("p b j -> p (b j)")
                        nc.tensor.matmul(o, xt_hi[rows, n, :], b_hi, start=True, stop=False)
                        nc.tensor.matmul(o, xt_lo[rows, n, :], b_hi, start=False, stop=False)
                        last = nc.tensor.matmul(o, xt_hi[rows, n, :], b_lo, start=False, stop=True)
                last.then_inc(g_mm, 1)

            bd_count = [None]

            def z2_field(s, j):
                def low():
                    nc.tensor.matmul(p_z2[:, 0:HID], g_lo[s][:, j, :], w1[:, j, 0:HID], start=False, stop=False)

                if j > 0:
                    low()
                wide = nc.tensor.matmul(p_z2[:, 0:2 * HID], g_hi[s][:, j, :], w1[:, j, :], start=(j == 0),
                                        stop=(j == FIELDS - 1))
                if j == 0:
                    low()
                if j == FIELDS - 1:
                    wide.then_inc(z2_mm, 1)

            def tile(t, s, first, last):
                for step in range(STEPS):
                    c, k = divmod(step, KT)
                    if k == 0:
                        embeddings_n(t, s, c, last)
                    if step + AHEAD < STEPS:
                        pair_sums(t, s, step + AHEAD)
                    elif not last:
                        if step + AHEAD == STEPS:
                            pe.wait_ge(et_out, cnt(t, 2, 4))
                        pair_sums((t[0], t[1] + 1), 1 - s, step + AHEAD - STEPS)
                    if not first and step >= Z2_FROM:
                        if step == Z2_FROM:
                            pe.wait_ge(g_l, cnt(t, 2 * CHUNKS))
                            ge(pe, z2_b, cnt(t, 1, -1))
                        for j in (2 * (step - Z2_FROM), 2 * (step - Z2_FROM) + 1):
                            if j < FIELDS:
                                z2_field(1 - s, j)
                    products(t, step)
                    if not (first and c == 0):
                        q = cnt(t, CHUNKS, c)
                        ps = (c - 1) % 2
                        x1_prev[0] = x1[ps]
                        bd_count[0] = cnt(t, 2 * 128, 128 * ((c + 1) // 2))
                        if k == XT_AT:
                            x1_transposed(q)
                        if k in G_AT:
                            g_half(q, ps, G_AT.index(k))
                    if step in ET_AT and not last:
                        pe.wait_ge(en_l, cnt(t, CHUNKS, c + 1))
                        embeddings_t((t[0], t[1] + 1), ET_AT.index(step), 1 - s)

            pe.wait_ge(prep, PREPARED)
            embeddings_t((None, 0), 0, 0)
            pe.wait_ge(et_out, 1)
            embeddings_t((None, 0), 1, 0)
            pe.wait_ge(et_out, 2)
            for step in range(AHEAD):
                pair_sums((None, 0), 0, step)
            over_tiles(pe, tile)

            q = TILES * CHUNKS
            x1_prev[0], bd_count[0] = x1[1], 2 * 128 * TILES
            x1_transposed(q)
            g_half(q, 1, 0)
            g_half(q, 1, 1)
            pe.wait_ge(g_l, 2 * q)
            pe.wait_ge(z2_b, TILES - 1)
            for j in range(FIELDS):
                z2_field(1, j)

            pe.wait_ge(top_in, 16 * 7)
            pe.wait_ge(z2_b, TILES)
            pe.wait_ge(z1_done, TILES)
            pe.wait_ge(xt_l, q)
            mlp_banks = [p_sum[0], p_sum[1], p_x1, p_misc]
            for blk in range(4):
                cols = slice(blk * 512, (blk + 1) * 512)
                for n in range(4):
                    last = nc.tensor.transpose(p_xt[:, n, :], z2_all[:, 4 * blk + n, :], ident[:, :])
                last.then_inc(tail_pe, 1)
                pe.wait_ge(tail_act, 8 * blk + 1)
                for m in range(4):
                    ms = slice(m * 128, (m + 1) * 128)
                    nc.tensor.matmul(mlp_banks[m][:, :], t_top1[:, 0, ms], z1_all[:, cols], start=True, stop=False)
                    nc.tensor.matmul(mlp_banks[m][:, :], t_top1[:, 1, ms], z2_t[:, :], start=False, stop=False)
                    nc.tensor.matmul(mlp_banks[m][:, :], t_top1d[:, ms], t_dense[:, cols], start=False,
                                     stop=True).then_inc(tail_pe, 1)
                for m in range(2):
                    ms = slice(m * 128, (m + 1) * 128)
                    for k in range(4):
                        pe.wait_ge(tail_act, 8 * blk + 2 + k)
                        last = nc.tensor.matmul(p_g[:, m, :], t_top2[:, k, ms], h1_sb[:, k, :], start=(k == 0),
                                                stop=(k == 3))
                    last.then_inc(tail_pe, 1)
                for k in range(2):
                    pe.wait_ge(tail_act, 8 * blk + 6 + k)
                    last = nc.tensor.matmul(p_z2[0:1, :], t_top3[:, k:k + 1], h2_sb[:, k, :], start=(k == 0), stop=(k == 1))
                last.then_inc(tail_pe, 1)

        @block.scalar
        def _(act):
            def square(t, step):
                act.wait_ge(sum_mm, cnt(t, STEPS, step + 1))
                ge(act, lo_done, cnt(t, STEPS, step - 1))
                rows = 128 if step % KT < FULL else REST_ROWS
                nc.scalar.activation(sq[step % 2][0:rows, :], p_sum[step % 2][0:rows, :], ACT.Square).then_inc(sq_done, 1)

            def transposed_out(n, s, r):
                act.wait_ge(et_mm, n)
                nc.scalar.copy(emb_t[s][:, :, 8 * r:8 * r + 8].rearrange("p b d -> p d b"),
                               p_misc_b[0:PARTS, :].rearrange("p (d b) -> p d b", b=TILE)).then_inc(et_out, 1)

            def x1_leaves(q, buf):
                act.wait_ge(prod_mm, q * KT)
                ge(act, xt_mm, q - 2)
                nc.scalar.copy(x1[buf][:, :], p_x1[:, :]).then_inc(x1_out, 1)

            def g_out(t_g, q, s, c, h):
                act.wait_ge(g_mm, q * 2 - 1 + h)
                if c == 0 and h == 0:
                    ge(act, z2_mm, t_g)
                    ge(act, z1_done, t_g)
                nc.scalar.copy(g_view(g_hi[s], c, h), g_bank_view()).then_inc(g_h, 1)

            def tile(t, s, first, last):
                for step in range(STEPS):
                    c, k = divmod(step, KT)
                    before = not (first and c == 0)
                    q = cnt(t, CHUNKS, c)
                    ps, pt = (c - 1) % 2, (s if c > 0 else 1 - s)
                    if k == 0 and before:
                        x1_leaves(q, ps)
                    if step + AHEAD < STEPS:
                        square(t, step + AHEAD)
                    elif not last:
                        square((t[0], t[1] + 1), step + AHEAD - STEPS)
                    if k == 0:
                        if not (first and c < 2):
                            pc = (c - 2) % CHUNKS
                            g_out(cnt(t, 1, -1 if c > 1 else -2), cnt(t, CHUNKS, c - 1), s if c > 1 else 1 - s, pc, 1)
                    if k == 1:
                        act.wait_ge(en_mm, cnt(t, CHUNKS, c + 1))
                        if not (first and c < 2):
                            act.wait_ge(bd_in[c % 2], cnt(t, 2 * 128, 128 * (c // 2)))
                        nc.scalar.copy(en[c % 2][:, 0, :, :], p_misc[:, 0:NT * GJ].rearrange("p (n j) -> p n j", j=GJ)).then_inc(en_h, 1)
                    if k == XT_AT + 1 and before:
                        act.wait_ge(xt_mm, q)
                        ge(act, g_mm, q * 2 - 2)
                        nc.scalar.copy(xt_hi[:, :, :], p_xt[:, :, :]).then_inc(xt_h, 1)
                    if k == G_AT[0] + 1 and before:
                        pc = (c - 1) % CHUNKS
                        g_out(cnt(t, 1, -1 if c > 0 else -2), q, pt, pc, 0)
                    if not last and step in (ET_AT[0] + 1, ET_AT[1] + 1):
                        r = ET_AT.index(step - 1)
                        transposed_out(cnt(t, 2, 3 + r), 1 - s, r)
                    if step == STEPS - 1 and not first:
                        act.wait_ge(z2_mm, cnt(t, 1))
                        ge(act, z2_b, cnt(t, 1, -1))
                        nc.scalar.copy(z2_part[:, :], p_z2[:, HID:2 * HID]).then_inc(z2_a, 1)

            transposed_out(1, 0, 0)
            transposed_out(2, 0, 1)
            for step in range(AHEAD):
                square((None, 0), step)
            over_tiles(act, tile)

            q = TILES * CHUNKS
            x1_leaves(q, 1)
            g_out(TILES - 2, q - 1, 1, 2, 1)
            act.wait_ge(xt_mm, q)
            act.wait_ge(g_mm, q * 2 - 2)
            nc.scalar.copy(xt_hi[:, :, :], p_xt[:, :, :]).then_inc(xt_h, 1)
            g_out(TILES - 2, q, 1, 3, 0)
            g_out(TILES - 2, q, 1, 3, 1)
            act.wait_ge(z2_mm, TILES)
            act.wait_ge(z2_b, TILES - 1)
            nc.scalar.copy(z2_part[:, :], p_z2[:, HID:2 * HID]).then_inc(z2_a, 1)

            mlp_banks = [p_sum[0], p_sum[1], p_x1, p_misc]
            act.wait_ge(top_in, 16 * 7)
            for blk in range(4):
                act.wait_ge(tail_pe, 8 * blk + 1)
                nc.scalar.copy(z2_t[:, :], p_xt[:, :, :].rearrange("p n h -> p (n h)")).then_inc(tail_act, 1)
                for m in range(4):
                    act.wait_ge(tail_pe, 8 * blk + 2 + m)
                    nc.scalar.activation(h1_sb[:, m, :], mlp_banks[m][:, :], ACT.Relu, bias=t_b1[:, m:m + 1]).then_inc(tail_act, 1)
                for m in range(2):
                    act.wait_ge(tail_pe, 8 * blk + 6 + m)
                    nc.scalar.activation(h2_sb[:, m, :], p_g[:, m, :], ACT.Relu, bias=t_b2[:, m:m + 1]).then_inc(tail_act, 1)
                act.wait_ge(tail_pe, 8 * blk + 8)
                nc.scalar.copy(y_sb[:, blk * 512:(blk + 1) * 512], p_z2[0:1, :]).then_inc(tail_act, 1)

        @block.vector
        def _(dve):
            done = [0]

            def chained(ins):
                ins.then_inc(prep, 1)
                done[0] += 1
                dve.wait_ge(prep, done[0])

            dve.wait_ge(consts_in, 16 * 8)
            nc.vector.tensor_copy(sel[:, :, :], r_sel[:, :, :]).then_inc(prep, 1)
            nc.vector.tensor_copy(sum3[:, :], r_sum3[:, :]).then_inc(prep, 1)
            nc.vector.tensor_copy(ident_b[:, :], ident[:, :]).then_inc(prep, 1)
            for s in range(2):
                nc.vector.tensor_copy(bd[s][:, :, :, :, :],
                                      r_diag[:, :, None, :, :].broadcast_to([128, 2, NT, QUAD, GJ])
                                      ).then_inc(prep, 1)
            done[0] = 5
            chained(nc.vector.tensor_tensor(r_pair[:, :, :], r_pair[:, :, :], r_swap[:, :, :], ALU.add))
            chained(nc.vector.tensor_reduce(r_tot[:, :], r_rows[:, :, :], AX.X, ALU.add))
            chained(nc.vector.tensor_scalar(r_tot[:, :], r_tot[:, :], -0.5, None, ALU.mult))
            chained(nc.vector.tensor_scalar(r_swap[:, :, :], r_pair[:, :, :], 0.5, None, ALU.mult))
            chained(nc.vector.tensor_tensor(r_swap[0:FIELDS, 0, :], r_pair[0:FIELDS, 0, :], r_tot[:, :], ALU.add))
            chained(nc.vector.tensor_copy(v_hi[:, :, :], r_swap[:, :, :]))
            nc.vector.tensor_tensor(v_lo[:, :, :], r_swap[:, :, :], v_hi[:, :, :], ALU.subtract).then_inc(prep, 1)
            nc.vector.tensor_copy(w1[:, :, 0:HID], r_w1[:, :, :]).then_inc(prep, 1)
            done[0] += 2
            dve.wait_ge(prep, done[0])
            rest = slice(64, REST_ROWS)
            nc.vector.tensor_tensor(v_hi[rest, FULL, :], r_swap[rest, FULL, :], v_hi[rest, FULL, :], ALU.subtract)
            nc.vector.tensor_tensor(w1[:, :, HID:2 * HID], r_w1[:, :, :], w1[:, :, 0:HID], ALU.subtract).then_inc(prep, 1)
            assert done[0] + 1 == PREPARED

            def split_parts(t, s, n):
                e = emb[s]
                out_part = lambda a: parts[:, :, a, :].rearrange("p d f -> p f d")
                if n == 0:
                    reg, at = t
                    dve.wait_ge(emb_in[s], 16 * FIELDS * (at // 2 + 1) if reg is None
                                else reg * (16 * FIELDS) + 16 * FIELDS * (at // 2 + 1))
                    ge(dve, et_mm, cnt(t, 2))
                    ge(dve, parts_done, cnt(t, 4))
                    nc.vector.tensor_copy(out_part(0), e[:, :, :]).then_inc(parts_done, 1)
                    return
                dve.wait_ge(parts_done, cnt(t, 4, n))
                if n == 1:
                    nc.vector.tensor_tensor(resid[:, :, :], e[:, :, :], out_part(0), ALU.subtract).then_inc(parts_done, 1)
                if n == 2:
                    nc.vector.tensor_copy(out_part(1), resid[:, :, :]).then_inc(parts_done, 1)
                if n == 3:
                    nc.vector.tensor_tensor(out_part(2), resid[:, :, :], out_part(1), ALU.subtract).then_inc(parts_done, 1)

            def high(t, step):
                r, a = step % 4, step % 2
                rows = 128 if step % KT < FULL else REST_ROWS
                dve.wait_ge(sq_done, cnt(t, STEPS, step + 1))
                ge(dve, prod_mm, cnt(t, STEPS, step - 3))
                nc.vector.tensor_copy(sq_hi[r][0:rows, :], sq[a][0:rows, :]).then_inc(hi_done, 1)

            def low(t, step):
                r, a = step % 4, step % 2
                dve.wait_ge(hi_done, cnt(t, STEPS, step + 1))
                if step % KT < FULL:
                    nc.vector.tensor_tensor(sq_lo[r][:, :], sq[a][:, :], sq_hi[r][:, :], ALU.subtract).then_inc(lo_done, 1)
                else:
                    mid = slice(32, 64)
                    nc.vector.tensor_tensor(sq_hi[r][mid, :], sq[a][mid, :], sq_hi[r][mid, :], ALU.subtract).then_inc(lo_done, 1)

            def g_low(n, s, c, h):
                dve.wait_ge(g_h, n)
                nc.vector.tensor_tensor(g_view(g_lo[s], c, h), g_bank_view(), g_view(g_hi[s], c, h),
                                        ALU.subtract).then_inc(g_l, 1)

            def xt_low(q):
                dve.wait_ge(xt_h, q)
                nc.vector.tensor_tensor(xt_lo[:, :, :], p_xt[:, :, :], xt_hi[:, :, :], ALU.subtract).then_inc(xt_l, 1)

            def z1_of(t_prev, s):
                reg, at = t_prev
                col = at * TILE if reg is None else reg * (2 * TILE) + at * TILE
                dve.wait_ge(g_l, cnt(t_prev, 2 * CHUNKS, 2 * CHUNKS))
                nc.vector.tensor_tensor(z1_all[:, bass.ds(col, TILE)], g_hi[s][:, FIELDS, :], g_lo[s][:, FIELDS, :],
                                        ALU.add).then_inc(z1_done, 1)

            def z2_of(t_prev):
                reg, at = t_prev
                dve.wait_ge(z2_a, cnt(t_prev, 1, 1))
                at = at if reg is None else reg * 2 + at
                nc.vector.tensor_tensor(z2_all[:, bass.ds(at, 1), :].rearrange("p a h -> p (a h)"), p_z2[:, 0:HID],
                                        z2_part[:, :], ALU.add).then_inc(z2_b, 1)

            def tile(t, s, first, last):
                for step in range(STEPS):
                    c, k = divmod(step, KT)
                    before = not (first and c == 0)
                    q = cnt(t, CHUNKS, c)
                    if step + AHEAD < STEPS:
                        high(t, step + AHEAD)
                        low(t, step + AHEAD)
                    elif not last:
                        high((t[0], t[1] + 1), step + AHEAD - STEPS)
                        low((t[0], t[1] + 1), step + AHEAD - STEPS)
                    if k == 0 and not (first and c < 2):
                        g_low(cnt(t, 2 * CHUNKS, 2 * (c - 1)), s if c > 1 else 1 - s, (c - 2) % CHUNKS, 1)
                    if k == 1:
                        dve.wait_ge(en_h, cnt(t, CHUNKS, c + 1))
                        nc.vector.tensor_tensor(en[c % 2][:, 1, :, :], p_misc[:, 0:NT * GJ].rearrange("p (n j) -> p n j", j=GJ),
                                                en[c % 2][:, 0, :, :], ALU.subtract).then_inc(en_l, 1)
                    if k == XT_AT + 1 and before:
                        xt_low(q)
                    if k == G_AT[0] + 1 and before:
                        g_low(cnt(t, 2 * CHUNKS, 2 * c - 1), s if c > 0 else 1 - s, (c - 1) % CHUNKS, 0)
                    if step == Z1_AT and not first:
                        z1_of((t[0], t[1] - 1), 1 - s)
                    if step in PARTS_AT and not last:
                        split_parts((t[0], t[1] + 1), 1 - s, PARTS_AT.index(step))
                    if step == STEPS - 1 and not first:
                        z2_of((t[0], t[1] - 1))

            for n in range(4):
                split_parts((None, 0), 0, n)
            for step in range(AHEAD):
                high((None, 0), step)
                low((None, 0), step)
            over_tiles(dve, tile)
            q = TILES * CHUNKS
            g_low(2 * q - 2, 1, 2, 1)
            xt_low(q)
            g_low(2 * q - 1, 1, 3, 0)
            g_low(2 * q, 1, 3, 1)
            z1_of((None, TILES - 1), 1)
            z2_of((None, TILES - 1))


def kernel(**inputs):
    import numpy as np
    import concourse.bacc as bacc
    from concourse.bass_utils import run_bass_kernel_spmd

    ids = np.asarray(inputs["ids"])
    ids = ids.reshape(BATCH // 32, 2, NT, QUAD, FIELDS).transpose(0, 2, 1, 3, 4).reshape(BATCH, FIELDS)

    pairs = [(i, i) for i in range(FIELDS)] + [(i, j) for i in range(FIELDS) for j in range(i + 1, FIELDS)]
    slots = [(n // 128, n % 128, n) for n in range(128 * FULL)]
    slots += [(FULL, at + n, 128 * FULL + n) for at in (0, 32, 64) for n in range(REST)]
    w0 = np.asarray(inputs["L0_rec_W0"]).reshape(HID, FIELDS, FIELDS)
    w0_pair = np.zeros((128, KT, HID), np.float32)
    w0_swap = np.zeros((128, KT, HID), np.float32)
    c_sel = np.zeros((PARTS, KT, 128), np.float32)
    for k, row, n in slots:
        i, j = pairs[n]
        w0_pair[row, k] = w0[:, i, j]
        w0_swap[row, k] = w0[:, j, i]
        for part in range(3):
            c_sel[part * FIELDS + i, k, row] = 1.0
            c_sel[part * FIELDS + j, k, row] = 1.0
    w0_rows = np.concatenate([w0.transpose(1, 0, 2), w0.transpose(2, 0, 1)], axis=2)
    c_sum3 = np.zeros((PARTS, GJ), np.float32)
    for n in range(PARTS):
        c_sum3[n, n % FIELDS] = 1.0
    c_diag = np.zeros((128, 2, QUAD, GJ), np.float32)
    for p in range(128):
        c_diag[p, 0, (p // DIM) % QUAD, FIELDS] = 1.0

    arrays = {
        "ids": ids, "w0_pair": w0_pair, "w0_swap": w0_swap, "w0_rows": w0_rows,
        "w1t": np.asarray(inputs["L0_rec_W1"]).reshape(HID, HID, FIELDS).transpose(1, 2, 0),
        "top1": inputs["W_top1"], "b1": np.asarray(inputs["b_top1"]).reshape(H1 // 128, 128).T,
        "top2": inputs["W_top2"], "b2": np.asarray(inputs["b_top2"]).reshape(H2 // 128, 128).T,
        "top3": np.asarray(inputs["W_top3"]).reshape(H2 // 128, 128).T,
        "dense_t": np.asarray(inputs["dense_ctx"]).T,
        "c_sel": c_sel, "c_sum3": c_sum3, "c_ident": np.eye(128, dtype=np.float32), "c_diag": c_diag,
    }
    for f in range(FIELDS):
        arrays[f"tbl_{f}"] = inputs[f"tbl_{f}"]
    nc = bacc.Bacc("TRN2", target_bir_lowering=False, num_devices=1)
    feed, ap = {}, {}
    for name, a in arrays.items():
        a = np.ascontiguousarray(a)
        feed[f"in_{name}"] = a
        ap[name] = nc.dram_tensor(f"in_{name}", a.shape, mybir.dt.from_np(a.dtype), kind="ExternalInput").ap()
    out = nc.dram_tensor("out_y", (1, BATCH), mybir.dt.float32, kind="ExternalOutput").ap()
    tables = [ap.pop(f"tbl_{f}") for f in range(FIELDS)]
    cin_tower_kernel(nc, tables=tables, out=out, **ap)
    r = run_bass_kernel_spmd(nc, [feed], core_ids=[0])
    return r.results[0]["out_y"].reshape(BATCH, 1)
```

```python
import concourse.bass as bass
from concourse import mybir
from contextlib import ExitStack

FIELDS, DIM, HID = 39, 16, 128
BATCH = 2048
TILE = 128
TILES = BATCH // TILE
CHUNKS = 4
COLS = TILE * DIM // CHUNKS
NT = COLS // 128
PARTS = 3 * FIELDS
PAIRS = FIELDS * (FIELDS + 1) // 2
FULL = PAIRS // 128
REST = PAIRS - 128 * FULL
KT = FULL + 1
REST_ROWS = 96
STEPS = CHUNKS * KT
AHEAD = 3
GJ = FIELDS + 1
EIGHT = 8
HI_ON_ACT = (1, 3, 5)
H1, H2 = 512, 256
BLOCK = 512
BLOCKS = BATCH // BLOCK
DENSE_ROWS = 80


def cin_tower_kernel(nc, ids, tables, w0_pair, w0_swap, w0_rows, w1t, top1, top1_dense, b1, top2, b2, top3, dense_t,
                     c_sel, c_sum3, c_ident, c_diag, out):
    fp32, bf16, f32r, i32 = mybir.dt.float32, mybir.dt.bfloat16, mybir.dt.float32r, mybir.dt.int32
    ALU = mybir.AluOpType
    ACT = mybir.ActivationFunctionType
    AX = mybir.AxisListType

    ctx = ExitStack()
    with ctx:
        def sb(name, shape, dt, where=ctx):
            return where.enter_context(nc.sbuf_tensor(name, shape, dt))

        def pb(name, shape, dt=fp32):
            return ctx.enter_context(nc.psum_tensor(name, shape, dt))

        def sem(name):
            return ctx.enter_context(nc.semaphore(name))

        sel = sb("sel", [PARTS, KT, 128], bf16)
        sum3 = sb("sum3", [PARTS, GJ], bf16)
        ident = sb("ident", [128, 128], fp32)
        ident_b = sb("ident_b", [128, 128], bf16)
        v_hi = sb("v_hi", [128, KT, HID], f32r)
        v_lo = sb("v_lo", [128, KT, HID], f32r)
        w1 = sb("w1", [128, FIELDS, 2 * HID], f32r)
        ids_sb = [sb(f"ids{s}", [128, FIELDS], i32) for s in range(2)]
        emb = [sb(f"emb{s}", [128, FIELDS, DIM], fp32) for s in range(2)]
        resid = sb("resid", [128, FIELDS, DIM], fp32)
        parts = sb("parts", [128, DIM, 3, FIELDS], bf16)
        emb_t = [sb(f"emb_t{s}", [PARTS, TILE, DIM], bf16) for s in range(2)]
        sq = [sb(f"sq{s}", [128, COLS], fp32) for s in range(4)]
        sq_hi = [sb(f"sq_hi{s}", [128, COLS], f32r) for s in range(4)]
        sq_lo = [sb(f"sq_lo{s}", [128, COLS], f32r) for s in range(4)]
        x1 = sb("x1", [128, COLS], fp32)
        xt_hi = sb("xt_hi", [128, NT, HID], f32r)
        xt_lo = sb("xt_lo", [128, NT, HID], f32r)
        en = [sb(f"en{s}", [128, 2, NT, GJ], f32r) for s in range(2)]
        bd = [sb(f"bd{s}", [128, 2, NT, EIGHT, GJ], f32r) for s in range(2)]
        z2_part = sb("z2_part", [128, HID], fp32)
        z2_sb = [sb(f"z2_sb{s}", [128, HID], fp32) for s in range(2)]
        b1_sb, b2_sb = sb("b1_sb", [128, H1 // 128], fp32), sb("b2_sb", [128, H2 // 128], fp32)
        top3_sb = sb("top3_sb", [128, H2 // 128], fp32)
        with ExitStack() as room:
            g_hi, g_lo = [], []
            for s in range(2):
                g_hi.append(sb(f"g_hi{s}", [128, GJ, TILE], f32r, room))
                g_lo.append(sb(f"g_lo{s}", [128, GJ, TILE], f32r, room))
        with ExitStack() as room:
            r_w1 = sb("r_w1", [128, FIELDS, HID], fp32, room)
            r_pair = sb("r_pair", [128, KT, HID], fp32, room)
            r_swap = sb("r_swap", [128, KT, HID], fp32, room)
            r_rows = sb("r_rows", [FIELDS, HID, 2 * FIELDS], fp32, room)
            r_sel = sb("r_sel", [PARTS, KT, 128], fp32, room)
            r_sum3 = sb("r_sum3", [PARTS, GJ], fp32, room)
            r_diag = sb("r_diag", [128, 2, EIGHT, GJ], fp32, room)
            r_tot = sb("r_tot", [FIELDS, HID], fp32, room)
            r_half = sb("r_half", [FIELDS, HID], fp32, room)
        with ExitStack() as room:
            t_top1 = sb("t_top1", [128, 2, H1], fp32, room)
            t_top2 = sb("t_top2", [128, H1 // 128, H2], fp32, room)
            t_top1d = sb("t_top1d", [DENSE_ROWS, H1], fp32, room)
            top1_hi = sb("top1_hi", [128, 2, H1], f32r, room)
            top1_lo = sb("top1_lo", [128, 2, H1], f32r, room)
            top2_hi = sb("top2_hi", [128, H1 // 128, H2], f32r, room)
            top2_lo = sb("top2_lo", [128, H1 // 128, H2], f32r, room)
            top1d = sb("top1d", [DENSE_ROWS, H1], f32r, room)
            z1_hi = [sb(f"z1_hi{s}", [128, BLOCK], f32r, room) for s in range(2)]
            z1_lo = [sb(f"z1_lo{s}", [128, BLOCK], f32r, room) for s in range(2)]
            z2_raw = [sb(f"z2_raw{s}", [128, NT, HID], fp32, room) for s in range(2)]
            t_dense = [sb(f"t_dense{s}", [DENSE_ROWS, BLOCK], fp32, room) for s in range(2)]
            dense = [sb(f"dense{s}", [DENSE_ROWS, BLOCK], f32r, room) for s in range(2)]
            z2_hi = sb("z2_hi", [128, BLOCK], f32r, room)
            z2_lo = sb("z2_lo", [128, BLOCK], f32r, room)
            h1_f = [sb(f"h1_f{s}", [128, BLOCK], fp32, room) for s in range(2)]
            h1_hi = sb("h1_hi", [128, H1 // 128, BLOCK], f32r, room)
            h1_lo = sb("h1_lo", [128, H1 // 128, BLOCK], f32r, room)
            h2_f = sb("h2_f", [128, H2 // 128, BLOCK], fp32, room)
            y_sb = sb("y_sb", [1, BLOCK], fp32, room)
        z1_dram = nc.dram_tensor("z1_dram", [2, 128, BATCH], fp32, kind="Internal").ap()
        z2_dram = nc.dram_tensor("z2_dram", [BATCH, HID], fp32, kind="Internal").ap()

        p_sum = [pb(f"p_sum{s}", [128, COLS]) for s in range(2)]
        p_x1 = pb("p_x1", [128, COLS])
        p_xt = pb("p_xt", [128, NT, HID])
        p_misc = pb("p_misc", [128, 512])
        p_misc_b = p_misc[:, :].bitcast(bf16)
        p_g = pb("p_g", [128, 2, 512])
        p_z2 = pb("p_z2", [128, 512])

        gather_begun = sem("gather_begun")
        consts_in, top_in, y_out = sem("consts_in"), sem("top_in"), sem("y_out")
        ids_in = [sem(f"ids_in{s}") for s in range(2)]
        emb_in = [sem(f"emb_in{s}") for s in range(2)]
        bd_in = [sem(f"bd_in{s}") for s in range(2)]
        prep = sem("prep")
        parts_done = sem("parts_done")
        et_mm, et_out = sem("et_mm"), sem("et_out")
        en_mm, en_h, en_l = sem("en_mm"), sem("en_h"), sem("en_l")
        sum_mm, sq_done, hi_done, lo_done, prod_mm = (sem(n) for n in ("sum_mm", "sq_done", "hi_done", "lo_done", "prod_mm"))
        x1_out, xt_mm, xt_h, xt_l = sem("x1_out"), sem("xt_mm"), sem("xt_h"), sem("xt_l")
        g_mm, g_h, g_l = sem("g_mm"), sem("g_h"), sem("g_l")
        z2_mm, z2_a, z2_b = sem("z2_mm"), sem("z2_a"), sem("z2_b")
        hi_act = sem("hi_act")
        z1_saved = [sem(f"z1_saved{s}") for s in range(2)]
        z2_saved = [sem(f"z2_saved{s}") for s in range(2)]
        block_in = [sem(f"block_in{s}") for s in range(2)]
        top_hi, top_ready, dense_ready, dense_hi = sem("top_hi"), sem("top_ready"), sem("dense_ready"), sem("dense_hi")
        zt_mm, zt_h, zt_l = sem("zt_mm"), sem("zt_h"), sem("zt_l")
        h1_mm, h1_relu, h1_h, h1_l = sem("h1_mm"), sem("h1_relu"), sem("h1_h"), sem("h1_l")
        h2_mm, h2_relu = sem("h2_mm"), sem("h2_relu")
        y_mm, y_copied = sem("y_mm"), sem("y_copied")

        PREPARED = 14
        TOP_READY = 4

        def g_view(buf, c, h):
            b = 32 * c + 16 * h
            return buf[:, :, b:b + 16].rearrange("p j (r m) -> p r m j", r=2)

        def g_bank_view():
            return p_g[:, :, 0:EIGHT * GJ].rearrange("p r (m j) -> p r m j", j=GJ)

        def cnt(t, per_tile, more=0):
            reg, at = t
            if reg is None:
                return per_tile * at + more
            return reg * (2 * per_tile) + (per_tile * at + more)

        def pair_cnt(t, per_two, more=0):
            reg, at = t
            if reg is None:
                return per_two * (at // 2) + more
            return reg * per_two + (per_two * (at // 2) + more)

        def row_of(t):
            reg, at = t
            return at * TILE if reg is None else reg * (2 * TILE) + at * TILE

        def hi_counts(step):
            by_act = sum((n % KT) in HI_ON_ACT for n in range(step + 1))
            return by_act, step + 1 - by_act

        def ge(eng, s, value):
            if not isinstance(value, int) or value > 0:
                eng.wait_ge(s, value)

        def over_tiles(eng, tile):
            tile((None, 0), 0, first=True, last=False)
            with eng.Fori(0, (TILES - 2) // 2) as i:
                tile((i, 1), 1, first=False, last=False)
                tile((i, 2), 0, first=False, last=False)
            tile((None, TILES - 1), 1, first=False, last=True)

        PARTS_AT = (KT + 3, KT + 4, KT + 6, 2 * KT)
        ET_AT = (2 * KT + 2, 2 * KT + 5)
        Z2_STEPS = range(KT + 3, STEPS - 1)
        XT_AT, G0_AT, G1_AT = 1, 4, 0

        block = ctx.enter_context(nc.Block())

        @block.sync
        def _(sp):
            def load_ids(t, s, after=None):
                row = row_of(t) if t[0] is None else sp.snap(row_of(t))
                if after is not None:
                    sp.wait_ge(emb_in[s], after)
                sp.dma_start(ids_sb[s][:, :], ids[bass.ds(row, TILE), :]).then_inc(ids_in[s], 16)

            load_ids((None, 0), 0)
            load_ids((None, 1), 1)
            for dst, src in ((r_sel[:, :, :], c_sel), (r_sum3[:, :], c_sum3), (ident[:, :], c_ident),
                             (r_diag[:, :, :, :], c_diag), (r_rows[:, :, :], w0_rows),
                             (r_pair[:, :, :], w0_pair), (r_swap[:, :, :], w0_swap), (r_w1[:, :, :], w1t), (b1_sb[:, :], b1),
                             (b2_sb[:, :], b2), (top3_sb[:, :], top3)):
                sp.dma_start(dst, src).then_inc(consts_in, 16)

            def before(t):
                return t[0], t[1] - 1

            def save_z1(t, s):
                row = row_of(t) if t[0] is None else sp.snap(row_of(t))
                for part, g in ((0, g_hi[s]), (1, g_lo[s])):
                    sp.dma_start(z1_dram[part, :, bass.ds(row, TILE)], g[:, FIELDS, :].bitcast(fp32)).then_inc(z1_saved[s], 16)

            def save_z2(t, s):
                row = row_of(t) if t[0] is None else sp.snap(row_of(t))
                sp.wait_ge(z2_b, cnt(t, 1, 1))
                sp.dma_start(z2_dram[bass.ds(row, TILE), :], z2_sb[s][:, :]).then_inc(z2_saved[s], 16)

            def load_block(n):
                s, cols = n % 2, slice(n * BLOCK, (n + 1) * BLOCK)
                for dst, src in ((z1_hi[s][:, :].bitcast(fp32), z1_dram[0, :, cols]),
                                 (z1_lo[s][:, :].bitcast(fp32), z1_dram[1, :, cols]),
                                 (z2_raw[s][:, :, :], z2_dram[cols, :].rearrange("(t p) h -> p t h", p=TILE)),
                                 (t_dense[s][:, :], dense_t[:, cols])):
                    sp.dma_start(dst, src).then_inc(block_in[s], 16)

            def tile(t, s, more, first=False):
                for c in range(CHUNKS):
                    cs = c % 2
                    if c == 1 and more:
                        load_ids((t[0], t[1] + 2), s, pair_cnt(t, 16 * FIELDS, 16 * FIELDS))
                    sp.wait_ge(en_l, cnt(t, CHUNKS, c + 1))
                    for b in range(8):
                        rows = slice(b * DIM, (b + 1) * DIM)
                        sp.dma_start(bd[cs][rows, :, :, b, 0:FIELDS].bitcast(fp32),
                                     en[cs][rows, :, :, 0:FIELDS].bitcast(fp32)).then_inc(bd_in[cs], 16)
                    if c == 1 and not first:
                        save_z1(before(t), 1 - s)
                if not first:
                    save_z2(before(t), 1 - s)

            sp.wait_ge(prep, PREPARED)
            tile((None, 0), 0, more=True, first=True)
            with sp.Fori(0, (TILES - 4) // 2) as i:
                tile((i, 1), 1, more=True)
                tile((i, 2), 0, more=True)
            tile((None, TILES - 3), 1, more=True)
            tile((None, TILES - 2), 0, more=False)
            tile((None, TILES - 1), 1, more=False)

            sp.wait_ge(z2_mm, TILES - 1)
            sp.wait_ge(z1_saved[0], 32 * TILES // 2)
            for dst, src in ((t_top1[:, :, :], top1.rearrange("(k p) n -> p k n", p=128)), (t_top1d[:, :], top1_dense),
                             (t_top2[:, :, :], top2.rearrange("(k p) n -> p k n", p=128))):
                sp.dma_start(dst, src).then_inc(top_in, 16)
            sp.wait_ge(g_l, 2 * CHUNKS * TILES)
            save_z1((None, TILES - 1), 1)
            sp.wait_ge(z1_saved[1], 32 * TILES // 2)
            sp.wait_ge(z2_mm, TILES)
            load_block(0)
            load_block(1)
            save_z2((None, TILES - 1), 1)
            sp.wait_ge(z2_saved[1], 16 * TILES // 2)
            for n in range(BLOCKS):
                if n + 2 < BLOCKS:
                    sp.wait_ge(h1_mm, 4 * (n + 1))
                    load_block(n + 2)
                sp.wait_ge(y_copied, n + 1)
                sp.dma_start(out[:, n * BLOCK:(n + 1) * BLOCK], y_sb[:, :]).then_inc(y_out, 16)
            sp.wait_ge(y_out, 16 * BLOCKS)

        @block.gpsimd
        def _(pool):
            def gather(t, s, first):
                if first:
                    pool.wait_ge(ids_in[s], 16)
                else:
                    pool.wait_ge(ids_in[s], t * 16 + 16)
                    pool.wait_ge(parts_done, t * 8 + (4 * s - 6))
                    pool.sem_inc(gather_begun, 1)
                for f in range(FIELDS):
                    nc.gpsimd.indirect_dma_start(
                        out=emb[s][:, f, :], out_offset=None, in_=tables[f],
                        in_offset=bass.IndirectOffsetOnAxis(ap=ids_sb[s][:, f:f + 1], axis=0)).then_inc(emb_in[s], 16)

            gather(0, 0, True)
            gather(0, 1, True)
            with pool.Fori(1, TILES // 2) as pair:
                gather(pair, 0, False)
                gather(pair, 1, False)

        @block.tensor
        def _(pe):
            def embeddings_t(t, r, s):
                pe.wait_ge(parts_done, cnt(t, 4, 4))
                for d in range(8):
                    last = nc.tensor.transpose(p_misc_b[0:PARTS, d * 128:(d + 1) * 128],
                                               parts[:, 8 * r + d, :, :].rearrange("p a f -> p (a f)"), ident_b[:, :])
                last.then_inc(et_mm, 1)

            def pair_sums(t, s, step):
                c, k = divmod(step, KT)
                ge(pe, sq_done, cnt(t, STEPS, step - 1))
                nc.tensor.matmul(p_sum[step % 2][:, :], sel[:, k, :],
                                 emb_t[s][:, c * 32:(c + 1) * 32, :].rearrange("p b d -> p (b d)"),
                                 start=True, stop=True).then_inc(sum_mm, 1)

            def products(t, step):
                c, k = divmod(step, KT)
                r = step % 4
                if k == 0:
                    ge(pe, x1_out, cnt(t, CHUNKS, c))
                pe.wait_ge(lo_done, cnt(t, STEPS, step + 1))
                if k < FULL:
                    nc.tensor.matmul(p_x1[:, :], v_hi[:, k, :], sq_hi[r][:, :], start=(k == 0), stop=False)
                    nc.tensor.matmul(p_x1[:, :], v_lo[:, k, :], sq_hi[r][:, :], start=False, stop=False)
                    nc.tensor.matmul(p_x1[:, :], v_hi[:, k, :], sq_lo[r][:, :], start=False, stop=False).then_inc(prod_mm, 1)
                else:
                    nc.tensor.matmul(p_x1[:, :], v_hi[0:REST_ROWS, k, :], sq_hi[r][0:REST_ROWS, :], start=False,
                                     stop=True).then_inc(prod_mm, 1)

            def embeddings_n(t, s, c, last):
                ge(pe, en_l, cnt(t, CHUNKS, c))
                if c == 0:
                    pe.wait_ge(et_out, cnt(t, 2, 2))
                if c == 3 and not last:
                    pe.wait_ge(et_out, cnt(t, 2, 4))
                for n in range(NT):
                    b = c * 32 + n * 8
                    mm = nc.tensor.matmul(p_misc[:, n * GJ:(n + 1) * GJ],
                                            emb_t[s][:, b:b + 8, :].rearrange("p b d -> p (b d)"), sum3[:, :],
                                            start=True, stop=True)
                mm.then_inc(en_mm, 1)

            def x1_transposed(q):
                pe.wait_ge(x1_out, q)
                ge(pe, xt_l, q - 1)
                for n in range(NT):
                    last = nc.tensor.transpose(p_xt[:, n, :], x1[:, n * 128:(n + 1) * 128], ident[:, :])
                last.then_inc(xt_mm, 1)

            def g_half(q, cs, h):
                if h == 0:
                    pe.wait_ge(xt_l, q)
                    pe.wait_ge(bd_in[cs], bd_count[0])
                ge(pe, g_l, q * 2 - 2 + h)
                for n in (2 * h, 2 * h + 1):
                    o = p_g[:, n % 2, 0:EIGHT * GJ]
                    b_hi = bd[cs][:, 0, n, :, :].rearrange("p b j -> p (b j)")
                    b_lo = bd[cs][:, 1, n, :, :].rearrange("p b j -> p (b j)")
                    nc.tensor.matmul(o, xt_hi[:, n, :], b_hi, start=True, stop=False)
                    nc.tensor.matmul(o, xt_lo[:, n, :], b_hi, start=False, stop=False)
                    last = nc.tensor.matmul(o, xt_hi[:, n, :], b_lo, start=False, stop=True)
                last.then_inc(g_mm, 1)

            bd_count = [None]

            def z2_field(s, j):
                def low():
                    nc.tensor.matmul(p_z2[:, 0:HID], g_lo[s][:, j, :], w1[:, j, 0:HID], start=False, stop=False)

                if j > 0:
                    low()
                wide = nc.tensor.matmul(p_z2[:, 0:2 * HID], g_hi[s][:, j, :], w1[:, j, :], start=(j == 0),
                                        stop=(j == FIELDS - 1))
                if j == 0:
                    low()
                if j == FIELDS - 1:
                    wide.then_inc(z2_mm, 1)

            def tile(t, s, first, last):
                for step in range(STEPS):
                    c, k = divmod(step, KT)
                    if k == 0:
                        embeddings_n(t, s, c, last)
                    if step + AHEAD < STEPS:
                        pair_sums(t, s, step + AHEAD)
                    elif not last:
                        if step + AHEAD == STEPS:
                            pe.wait_ge(et_out, cnt(t, 2, 4))
                        pair_sums((t[0], t[1] + 1), 1 - s, step + AHEAD - STEPS)
                    if not first and step in Z2_STEPS:
                        n = step - Z2_STEPS[0]
                        if n == 0:
                            pe.wait_ge(g_l, cnt(t, 2 * CHUNKS))
                            ge(pe, z2_b, cnt(t, 1, -1))
                        for j in range(FIELDS * n // len(Z2_STEPS), FIELDS * (n + 1) // len(Z2_STEPS)):
                            z2_field(1 - s, j)
                    if k == G1_AT and not (first and c < 2):
                        g_half(cnt(t, CHUNKS, c - 1), c % 2, 1)
                    products(t, step)
                    if not (first and c == 0):
                        q = cnt(t, CHUNKS, c)
                        ps = (c - 1) % 2
                        bd_count[0] = cnt(t, 2 * 128, 128 * ((c + 1) // 2))
                        if k == XT_AT:
                            x1_transposed(q)
                        if k == G0_AT:
                            g_half(q, ps, 0)
                    if step in ET_AT and not last:
                        pe.wait_ge(en_l, cnt(t, CHUNKS, c + 1))
                        pe.wait_ge(et_out, cnt(t, 2, 2 + ET_AT.index(step)))
                        embeddings_t((t[0], t[1] + 1), ET_AT.index(step), 1 - s)

            pe.wait_ge(prep, PREPARED)
            embeddings_t((None, 0), 0, 0)
            pe.wait_ge(et_out, 1)
            embeddings_t((None, 0), 1, 0)
            pe.wait_ge(et_out, 2)
            for step in range(AHEAD):
                pair_sums((None, 0), 0, step)
            over_tiles(pe, tile)

            q = TILES * CHUNKS
            bd_count[0] = 2 * 128 * TILES
            g_half(q - 1, 0, 1)
            x1_transposed(q)
            g_half(q, 1, 0)
            g_half(q, 1, 1)
            pe.wait_ge(g_l, 2 * q)
            pe.wait_ge(z2_b, TILES - 1)
            for j in range(FIELDS):
                z2_field(1, j)

            h1_banks = [p_sum[0], p_sum[1], p_x1, p_misc]

            def z2_transposed(n):
                pe.wait_ge(block_in[n % 2], 64 * (n // 2 + 1))
                pe.wait_ge(xt_l, q)
                ge(pe, zt_l, n)
                for i in range(NT):
                    last = nc.tensor.transpose(p_xt[:, i, :], z2_raw[n % 2][:, i, :], ident[:, :])
                last.then_inc(zt_mm, 1)

            def layer1(n):
                s = n % 2
                pe.wait_ge(dense_ready, n + 1)
                pe.wait_ge(zt_l, n + 1)
                for m in range(H1 // 128):
                    ms = slice(m * 128, (m + 1) * 128)
                    o = h1_banks[m][:, :]
                    ge(pe, h1_h, 4 * (n - 1) + m + 1)
                    nc.tensor.matmul(o, top1d[:, ms], dense[s][:, :], start=True, stop=False)
                    for k, (z_hi, z_lo) in enumerate(((z1_hi[s], z1_lo[s]), (z2_hi, z2_lo))):
                        nc.tensor.matmul(o, top1_hi[:, k, ms], z_hi[:, :], start=False, stop=False)
                        nc.tensor.matmul(o, top1_lo[:, k, ms], z_hi[:, :], start=False, stop=False)
                        last = nc.tensor.matmul(o, top1_hi[:, k, ms], z_lo[:, :], start=False, stop=(k == 1))
                    last.then_inc(h1_mm, 1)

            def layer2(n):
                for m in range(H2 // 128):
                    ms = slice(m * 128, (m + 1) * 128)
                    ge(pe, h2_relu, 2 * (n - 1) + m + 1)
                    for k in range(H1 // 128):
                        pe.wait_ge(h1_l, 4 * n + k + 1)
                        nc.tensor.matmul(p_g[:, m, :], top2_hi[:, k, ms], h1_hi[:, k, :], start=(k == 0), stop=False)
                        nc.tensor.matmul(p_g[:, m, :], top2_lo[:, k, ms], h1_hi[:, k, :], start=False, stop=False)
                        last = nc.tensor.matmul(p_g[:, m, :], top2_hi[:, k, ms], h1_lo[:, k, :], start=False,
                                                stop=(k == H1 // 128 - 1))
                    last.then_inc(h2_mm, 1)

            def layer3(n):
                ge(pe, y_copied, n)
                for k in range(H2 // 128):
                    pe.wait_ge(h2_relu, 2 * n + k + 1)
                    last = nc.tensor.matmul(p_z2[0:1, :], top3_sb[:, k:k + 1], h2_f[:, k, :], start=(k == 0),
                                            stop=(k == H2 // 128 - 1))
                last.then_inc(y_mm, 1)

            pe.wait_ge(top_ready, TOP_READY)
            pe.wait_ge(z2_b, TILES)
            z2_transposed(0)
            for n in range(BLOCKS):
                layer1(n)
                if n + 1 < BLOCKS:
                    z2_transposed(n + 1)
                if n > 0:
                    layer3(n - 1)
                layer2(n)
            layer3(BLOCKS - 1)

        @block.scalar
        def _(act):
            def square(t, step):
                act.wait_ge(sum_mm, cnt(t, STEPS, step + 1))
                ge(act, lo_done, cnt(t, STEPS, step - 3))
                rows = 128 if step % KT < FULL else REST_ROWS
                if step % KT in HI_ON_ACT:
                    ge(act, prod_mm, cnt(t, STEPS, step - 3))
                    nc.scalar.activation(sq_hi[step % 4][0:rows, :], p_sum[step % 2][0:rows, :], ACT.Square).then_inc(hi_act, 1)
                nc.scalar.activation(sq[step % 4][0:rows, :], p_sum[step % 2][0:rows, :], ACT.Square).then_inc(sq_done, 1)

            def transposed_out(n, s, r):
                act.wait_ge(et_mm, n)
                nc.scalar.copy(emb_t[s][:, :, 8 * r:8 * r + 8].rearrange("p b d -> p d b"),
                               p_misc_b[0:PARTS, :].rearrange("p (d b) -> p d b", b=TILE)).then_inc(et_out, 1)

            def x1_leaves(q):
                act.wait_ge(prod_mm, q * KT)
                ge(act, xt_mm, q - 1)
                nc.scalar.copy(x1[:, :], p_x1[:, :]).then_inc(x1_out, 1)

            def g_out(t_g, q, s, c, h):
                act.wait_ge(g_mm, q * 2 - 1 + h)
                if c == 0 and h == 0:
                    ge(act, z2_mm, cnt(t_g, 1, -1))
                    if t_g[0] is not None or t_g[1] > 1:
                        act.wait_ge(z1_saved[s], pair_cnt(t_g, 32))
                nc.scalar.copy(g_view(g_hi[s], c, h), g_bank_view()).then_inc(g_h, 1)

            def tile(t, s, first, last):
                for step in range(STEPS):
                    c, k = divmod(step, KT)
                    before = not (first and c == 0)
                    q = cnt(t, CHUNKS, c)
                    pt = s if c > 0 else 1 - s
                    if k == 0 and before:
                        x1_leaves(q)
                    if k == G1_AT + 1 and not (first and c < 2):
                        g_out(t, cnt(t, CHUNKS, c - 1), s if c > 1 else 1 - s, (c - 2) % CHUNKS, 1)
                    if k == 1:
                        act.wait_ge(en_mm, cnt(t, CHUNKS, c + 1))
                        if not (first and c < 2):
                            act.wait_ge(bd_in[c % 2], cnt(t, 2 * 128, 128 * (c // 2)))
                        nc.scalar.copy(en[c % 2][:, 0, :, :], p_misc[:, 0:NT * GJ].rearrange("p (n j) -> p n j", j=GJ)).then_inc(en_h, 1)
                    if k == XT_AT + 1 and before:
                        act.wait_ge(xt_mm, q)
                        ge(act, g_mm, q * 2 - 2)
                        nc.scalar.copy(xt_hi[:, :, :], p_xt[:, :, :]).then_inc(xt_h, 1)
                    if k == G0_AT + 1 and before:
                        g_out(t, q, pt, (c - 1) % CHUNKS, 0)
                    if step + AHEAD < STEPS:
                        square(t, step + AHEAD)
                    elif not last:
                        square((t[0], t[1] + 1), step + AHEAD - STEPS)
                    if not last and step in (ET_AT[0] + 1, ET_AT[1] + 1):
                        r = ET_AT.index(step - 1)
                        transposed_out(cnt(t, 2, 3 + r), 1 - s, r)
                    if step == STEPS - 1 and not first:
                        act.wait_ge(z2_mm, cnt(t, 1))
                        ge(act, z2_b, cnt(t, 1, -1))
                        nc.scalar.copy(z2_part[:, :], p_z2[:, HID:2 * HID]).then_inc(z2_a, 1)

            transposed_out(1, 0, 0)
            transposed_out(2, 0, 1)
            for step in range(AHEAD):
                square((None, 0), step)
            over_tiles(act, tile)

            q = TILES * CHUNKS
            x1_leaves(q)
            g_out((None, TILES - 1), q - 1, 1, 2, 1)
            act.wait_ge(xt_mm, q)
            act.wait_ge(g_mm, q * 2 - 2)
            nc.scalar.copy(xt_hi[:, :, :], p_xt[:, :, :]).then_inc(xt_h, 1)
            g_out((None, TILES - 1), q, 1, 3, 0)
            g_out((None, TILES - 1), q, 1, 3, 1)
            act.wait_ge(top_in, 16 * 3)
            nc.scalar.copy(top1_hi[:, :, :], t_top1[:, :, :]).then_inc(top_hi, 1)
            nc.scalar.copy(top2_hi[:, :, :], t_top2[:, :, :]).then_inc(top_hi, 1)
            act.wait_ge(z2_mm, TILES)
            act.wait_ge(z2_b, TILES - 1)
            nc.scalar.copy(z2_part[:, :], p_z2[:, HID:2 * HID]).then_inc(z2_a, 1)

            h1_banks = [p_sum[0], p_sum[1], p_x1, p_misc]

            def z2_high(n):
                act.wait_ge(zt_mm, n + 1)
                ge(act, h1_mm, 4 * n)
                nc.scalar.copy(z2_hi[:, :], p_xt[:, :, :].rearrange("p n h -> p (n h)")).then_inc(zt_h, 1)

            def layer3_out(n):
                act.wait_ge(y_mm, n + 1)
                ge(act, y_out, 16 * n)
                nc.scalar.copy(y_sb[:, :], p_z2[0:1, :]).then_inc(y_copied, 1)

            z2_high(0)
            for n in range(BLOCKS):
                for m in range(H1 // 128):
                    act.wait_ge(h1_mm, 4 * n + m + 1)
                    ge(act, h2_mm, 2 * n)
                    ge(act, h1_l, 4 * n + m - 1)
                    nc.scalar.activation(h1_f[m % 2][:, :], h1_banks[m][:, :], ACT.Relu, bias=b1_sb[:, m:m + 1]).then_inc(h1_relu, 1)
                    nc.scalar.activation(h1_hi[:, m, :], h1_banks[m][:, :], ACT.Relu, bias=b1_sb[:, m:m + 1]).then_inc(h1_h, 1)
                if n + 1 < BLOCKS:
                    z2_high(n + 1)
                if n > 0:
                    layer3_out(n - 1)
                for m in range(H2 // 128):
                    act.wait_ge(h2_mm, 2 * n + m + 1)
                    ge(act, y_mm, n)
                    nc.scalar.activation(h2_f[:, m, :], p_g[:, m, :], ACT.Relu, bias=b2_sb[:, m:m + 1]).then_inc(h2_relu, 1)
            layer3_out(BLOCKS - 1)

        @block.vector
        def _(dve):
            done = [0]

            def chained(ins):
                ins.then_inc(prep, 1)
                done[0] += 1
                dve.wait_ge(prep, done[0])

            dve.wait_ge(consts_in, 16 * 11)
            nc.vector.tensor_copy(sel[:, :, :], r_sel[:, :, :]).then_inc(prep, 1)
            nc.vector.tensor_copy(sum3[:, :], r_sum3[:, :]).then_inc(prep, 1)
            nc.vector.tensor_copy(ident_b[:, :], ident[:, :]).then_inc(prep, 1)
            for s in range(2):
                nc.vector.tensor_copy(bd[s][:, :, :, :, :],
                                      r_diag[:, :, None, :, :].broadcast_to([128, 2, NT, EIGHT, GJ])
                                      ).then_inc(prep, 1)
            done[0] = 5
            chained(nc.vector.tensor_tensor(r_pair[:, :, :], r_pair[:, :, :], r_swap[:, :, :], ALU.add))
            chained(nc.vector.tensor_reduce(r_tot[:, :], r_rows[:, :, :], AX.X, ALU.add))
            chained(nc.vector.tensor_scalar(r_tot[:, :], r_tot[:, :], -0.5, None, ALU.mult))
            chained(nc.vector.tensor_scalar(r_swap[:, :, :], r_pair[:, :, :], 0.5, None, ALU.mult))
            chained(nc.vector.tensor_tensor(r_swap[0:FIELDS, 0, :], r_pair[0:FIELDS, 0, :], r_tot[:, :], ALU.add))
            chained(nc.vector.tensor_copy(v_hi[:, :, :], r_swap[:, :, :]))
            nc.vector.tensor_tensor(v_lo[:, :, :], r_swap[:, :, :], v_hi[:, :, :], ALU.subtract).then_inc(prep, 1)
            nc.vector.tensor_copy(w1[:, :, 0:HID], r_w1[:, :, :]).then_inc(prep, 1)
            done[0] += 2
            dve.wait_ge(prep, done[0])
            rest = slice(64, REST_ROWS)
            nc.vector.tensor_tensor(v_hi[rest, FULL, :], r_swap[rest, FULL, :], v_hi[rest, FULL, :], ALU.subtract)
            nc.vector.tensor_tensor(w1[:, :, HID:2 * HID], r_w1[:, :, :], w1[:, :, 0:HID], ALU.subtract).then_inc(prep, 1)
            assert done[0] + 1 == PREPARED

            def split_parts(t, s, n):
                e = emb[s]
                out_part = lambda a: parts[:, :, a, :].rearrange("p d f -> p f d")
                if n == 0:
                    dve.wait_ge(emb_in[s], pair_cnt(t, 16 * FIELDS, 16 * FIELDS))
                    ge(dve, et_mm, cnt(t, 2))
                    ge(dve, parts_done, cnt(t, 4))
                    nc.vector.tensor_copy(out_part(0), e[:, :, :]).then_inc(parts_done, 1)
                    return
                dve.wait_ge(parts_done, cnt(t, 4, n))
                if n == 1:
                    nc.vector.tensor_tensor(resid[:, :, :], e[:, :, :], out_part(0), ALU.subtract).then_inc(parts_done, 1)
                if n == 2:
                    nc.vector.tensor_copy(out_part(1), resid[:, :, :]).then_inc(parts_done, 1)
                if n == 3:
                    nc.vector.tensor_tensor(out_part(2), resid[:, :, :], out_part(1), ALU.subtract).then_inc(parts_done, 1)

            def high(t, step):
                r = step % 4
                rows = 128 if step % KT < FULL else REST_ROWS
                if step % KT not in HI_ON_ACT:
                    dve.wait_ge(sq_done, cnt(t, STEPS, step + 1))
                    ge(dve, prod_mm, cnt(t, STEPS, step - 3))
                    nc.vector.tensor_copy(sq_hi[r][0:rows, :], sq[r][0:rows, :]).then_inc(hi_done, 1)

            def low(t, step):
                r = step % 4
                by_act, by_dve = hi_counts(step)
                all_act, all_dve = hi_counts(STEPS - 1)
                if step % KT in HI_ON_ACT:
                    dve.wait_ge(hi_act, cnt(t, all_act, by_act))
                    dve.wait_ge(sq_done, cnt(t, STEPS, step + 1))
                    ge(dve, prod_mm, cnt(t, STEPS, step - 3))
                else:
                    dve.wait_ge(hi_done, cnt(t, all_dve, by_dve))
                if step % KT < FULL:
                    nc.vector.tensor_tensor(sq_lo[r][:, :], sq[r][:, :], sq_hi[r][:, :], ALU.subtract).then_inc(lo_done, 1)
                else:
                    mid = slice(32, 64)
                    nc.vector.tensor_tensor(sq_hi[r][mid, :], sq[r][mid, :], sq_hi[r][mid, :], ALU.subtract).then_inc(lo_done, 1)

            def g_low(n, s, c, h):
                dve.wait_ge(g_h, n)
                nc.vector.tensor_tensor(g_view(g_lo[s], c, h), g_bank_view(), g_view(g_hi[s], c, h),
                                        ALU.subtract).then_inc(g_l, 1)

            def xt_low(q):
                dve.wait_ge(xt_h, q)
                nc.vector.tensor_tensor(xt_lo[:, :, :], p_xt[:, :, :], xt_hi[:, :, :], ALU.subtract).then_inc(xt_l, 1)

            def z2_of(t, s):
                dve.wait_ge(z2_a, cnt(t, 1, 1))
                if t[0] is not None or t[1] > 1:
                    ge(dve, z2_saved[s], pair_cnt(t, 16))
                nc.vector.tensor_tensor(z2_sb[s][:, :], p_z2[:, 0:HID], z2_part[:, :], ALU.add).then_inc(z2_b, 1)

            def tile(t, s, first, last):
                for step in range(STEPS):
                    c, k = divmod(step, KT)
                    before = not (first and c == 0)
                    q = cnt(t, CHUNKS, c)
                    if k == G1_AT + 1 and not (first and c < 2):
                        g_low(cnt(t, 2 * CHUNKS, 2 * (c - 1)), s if c > 1 else 1 - s, (c - 2) % CHUNKS, 1)
                    if k == 1:
                        dve.wait_ge(en_h, cnt(t, CHUNKS, c + 1))
                        nc.vector.tensor_tensor(en[c % 2][:, 1, :, :], p_misc[:, 0:NT * GJ].rearrange("p (n j) -> p n j", j=GJ),
                                                en[c % 2][:, 0, :, :], ALU.subtract).then_inc(en_l, 1)
                    if k == XT_AT + 1 and before:
                        xt_low(q)
                    if k == G0_AT + 1 and before:
                        g_low(cnt(t, 2 * CHUNKS, 2 * c - 1), s if c > 0 else 1 - s, (c - 1) % CHUNKS, 0)
                    if step + AHEAD < STEPS:
                        high(t, step + AHEAD)
                        low(t, step + AHEAD)
                    elif not last:
                        high((t[0], t[1] + 1), step + AHEAD - STEPS)
                        low((t[0], t[1] + 1), step + AHEAD - STEPS)
                    if step in PARTS_AT and not last:
                        split_parts((t[0], t[1] + 1), 1 - s, PARTS_AT.index(step))
                    if step == STEPS - 1 and not first:
                        z2_of((t[0], t[1] - 1), 1 - s)

            for n in range(4):
                split_parts((None, 0), 0, n)
            for step in range(AHEAD):
                high((None, 0), step)
                low((None, 0), step)
            over_tiles(dve, tile)
            q = TILES * CHUNKS
            g_low(2 * q - 2, 1, 2, 1)
            xt_low(q)
            g_low(2 * q - 1, 1, 3, 0)
            g_low(2 * q, 1, 3, 1)
            dve.wait_ge(top_in, 16 * 3)
            nc.vector.tensor_copy(top1d[:, :], t_top1d[:, :]).then_inc(top_ready, 1)
            dve.wait_ge(top_ready, 1)
            low_rows = slice(64, DENSE_ROWS)
            nc.vector.tensor_tensor(top1d[low_rows, :], t_top1d[low_rows, :], top1d[low_rows, :], ALU.subtract).then_inc(top_ready, 1)
            dve.wait_ge(top_hi, 1)
            nc.vector.tensor_tensor(top1_lo[:, :, :], t_top1[:, :, :], top1_hi[:, :, :], ALU.subtract).then_inc(top_ready, 1)
            dve.wait_ge(top_hi, 2)
            nc.vector.tensor_tensor(top2_lo[:, :, :], t_top2[:, :, :], top2_hi[:, :, :], ALU.subtract).then_inc(top_ready, 1)
            z2_of((None, TILES - 1), 1)

            def dense_parts(n):
                s, low_rows = n % 2, slice(32, 64)
                dve.wait_ge(block_in[s], 64 * (n // 2 + 1))
                nc.vector.tensor_copy(dense[s][:, :], t_dense[s][:, :]).then_inc(dense_hi, 1)
                dve.wait_ge(dense_hi, n + 1)
                nc.vector.tensor_tensor(dense[s][low_rows, :], t_dense[s][low_rows, :], dense[s][low_rows, :],
                                        ALU.subtract).then_inc(dense_ready, 1)

            def z2_low(n):
                dve.wait_ge(zt_h, n + 1)
                nc.vector.tensor_tensor(z2_lo[:, :], p_xt[:, :, :].rearrange("p n h -> p (n h)"), z2_hi[:, :],
                                        ALU.subtract).then_inc(zt_l, 1)

            dense_parts(0)
            z2_low(0)
            for n in range(BLOCKS):
                for m in range(H1 // 128):
                    dve.wait_ge(h1_relu, 4 * n + m + 1)
                    dve.wait_ge(h1_h, 4 * n + m + 1)
                    nc.vector.tensor_tensor(h1_lo[:, m, :], h1_f[m % 2][:, :], h1_hi[:, m, :], ALU.subtract).then_inc(h1_l, 1)
                if n + 1 < BLOCKS:
                    dense_parts(n + 1)
                    z2_low(n + 1)


def kernel(**inputs):
    import numpy as np
    import concourse.bacc as bacc
    from concourse.bass_utils import run_bass_kernel_spmd

    pairs = [(i, i) for i in range(FIELDS)] + [(i, j) for i in range(FIELDS) for j in range(i + 1, FIELDS)]
    slots = [(n // 128, n % 128, n) for n in range(128 * FULL)]
    slots += [(FULL, at + n, 128 * FULL + n) for at in (0, 32, 64) for n in range(REST)]
    w0 = np.asarray(inputs["L0_rec_W0"]).reshape(HID, FIELDS, FIELDS)
    w0_pair = np.zeros((128, KT, HID), np.float32)
    w0_swap = np.zeros((128, KT, HID), np.float32)
    c_sel = np.zeros((PARTS, KT, 128), np.float32)
    for k, row, n in slots:
        i, j = pairs[n]
        w0_pair[row, k] = w0[:, i, j]
        w0_swap[row, k] = w0[:, j, i]
        for part in range(3):
            c_sel[part * FIELDS + i, k, row] = 1.0
            c_sel[part * FIELDS + j, k, row] = 1.0
    w0_rows = np.concatenate([w0.transpose(1, 0, 2), w0.transpose(2, 0, 1)], axis=2)
    c_sum3 = np.zeros((PARTS, GJ), np.float32)
    for n in range(PARTS):
        c_sum3[n, n % FIELDS] = 1.0
    c_diag = np.zeros((128, 2, EIGHT, GJ), np.float32)
    for p in range(128):
        c_diag[p, 0, p // DIM, FIELDS] = 1.0
    top1 = np.asarray(inputs["W_top1"])
    top1_dense = np.zeros((DENSE_ROWS, H1), np.float32)
    dense_t = np.zeros((DENSE_ROWS, BATCH), np.float32)
    for at in (0, 32, 64):
        top1_dense[at:at + DIM] = top1[2 * HID:]
        dense_t[at:at + DIM] = np.asarray(inputs["dense_ctx"]).T

    arrays = {
        "ids": inputs["ids"], "w0_pair": w0_pair, "w0_swap": w0_swap, "w0_rows": w0_rows,
        "w1t": np.asarray(inputs["L0_rec_W1"]).reshape(HID, HID, FIELDS).transpose(1, 2, 0),
        "top1": top1[:2 * HID], "top1_dense": top1_dense, "b1": np.asarray(inputs["b_top1"]).reshape(H1 // 128, 128).T,
        "top2": inputs["W_top2"], "b2": np.asarray(inputs["b_top2"]).reshape(H2 // 128, 128).T,
        "top3": np.asarray(inputs["W_top3"]).reshape(H2 // 128, 128).T,
        "dense_t": dense_t,
        "c_sel": c_sel, "c_sum3": c_sum3, "c_ident": np.eye(128, dtype=np.float32), "c_diag": c_diag,
    }
    for f in range(FIELDS):
        arrays[f"tbl_{f}"] = inputs[f"tbl_{f}"]
    nc = bacc.Bacc("TRN2", target_bir_lowering=False, num_devices=1)
    feed, ap = {}, {}
    for name, a in arrays.items():
        a = np.ascontiguousarray(a)
        feed[f"in_{name}"] = a
        ap[name] = nc.dram_tensor(f"in_{name}", a.shape, mybir.dt.from_np(a.dtype), kind="ExternalInput").ap()
    out = nc.dram_tensor("out_y", (1, BATCH), mybir.dt.float32, kind="ExternalOutput").ap()
    tables = [ap.pop(f"tbl_{f}") for f in range(FIELDS)]
    cin_tower_kernel(nc, tables=tables, out=out, **ap)
    r = run_bass_kernel_spmd(nc, [feed], core_ids=[0])
    return r.results[0]["out_y"].reshape(BATCH, 1)
```

```python
import concourse.bass as bass
from concourse import mybir
from contextlib import ExitStack

FIELDS, DIM, HID = 39, 16, 128
BATCH = 2048
TILE = 128
TILES = BATCH // TILE
CHUNKS = 4
COLS = TILE * DIM // CHUNKS
NT = COLS // 128
PARTS = 3 * FIELDS
PAIRS = FIELDS * (FIELDS + 1) // 2
FULL = PAIRS // 128
REST = PAIRS - 128 * FULL
KT = FULL + 1
REST_ROWS = 96
STEPS = CHUNKS * KT
AHEAD = 3
GJ = FIELDS + 1
EIGHT = 8
HI_ON_ACT = (1, 3, 4)
H1, H2 = 512, 256
BLOCK = 512
BLOCKS = BATCH // BLOCK
GATE = FIELDS // 2 + 1
DENSE_ROWS = 80


def cin_tower_kernel(nc, ids, tables, w0_pair, w0_swap, w0_rows, w1t, top1, top1_dense, b1, top2, b2, top3, dense_t,
                     c_sel, c_sum3, c_ident, c_diag, out):
    fp32, bf16, f32r, i32 = mybir.dt.float32, mybir.dt.bfloat16, mybir.dt.float32r, mybir.dt.int32
    ALU = mybir.AluOpType
    ACT = mybir.ActivationFunctionType
    AX = mybir.AxisListType

    ctx = ExitStack()
    with ctx:
        def sb(name, shape, dt, where=ctx):
            return where.enter_context(nc.sbuf_tensor(name, shape, dt))

        def pb(name, shape, dt=fp32):
            return ctx.enter_context(nc.psum_tensor(name, shape, dt))

        def sem(name):
            return ctx.enter_context(nc.semaphore(name))

        sel = sb("sel", [PARTS, KT, 128], bf16)
        sum3 = sb("sum3", [PARTS, GJ], bf16)
        ident = sb("ident", [128, 128], fp32)
        ident_b = sb("ident_b", [128, 128], bf16)
        v_hi = sb("v_hi", [128, KT, HID], f32r)
        v_lo = sb("v_lo", [128, KT, HID], f32r)
        w1 = sb("w1", [128, FIELDS, 2 * HID], f32r)
        ids_sb = [sb(f"ids{s}", [128, FIELDS], i32) for s in range(2)]
        emb = [sb(f"emb{s}", [128, FIELDS, DIM], fp32) for s in range(2)]
        with ExitStack() as room:
            z1_hi = [sb("z1_hi0", [128, BLOCK], f32r, room)]
        resid = sb("resid", [128, FIELDS, DIM], fp32)
        with ExitStack() as room:
            z1_lo = [sb("z1_lo0", [128, BLOCK], f32r, room)]
        parts = sb("parts", [128, DIM, 3, FIELDS], bf16)
        emb_t, t_dense = [], []
        for s in range(2):
            with ExitStack() as room:
                t_dense.append(sb(f"t_dense{s}", [DENSE_ROWS, BLOCK], fp32, room))
            emb_t.append(sb(f"emb_t{s}", [PARTS, TILE, DIM], bf16))
        with ExitStack() as room:
            z2_hi = sb("z2_hi", [128, BLOCK], f32r, room)
            z2_lo = sb("z2_lo", [128, BLOCK], f32r, room)
            dense = [sb(f"dense{s}", [DENSE_ROWS, BLOCK], f32r, room) for s in range(2)]
            h1_hi = sb("h1_hi", [128, H1 // 128, BLOCK], f32r, room)
            h1_lo = sb("h1_lo", [128, H1 // 128, BLOCK], f32r, room)
            h2_f = sb("h2_f", [128, H2 // 128, BLOCK], fp32, room)
        with ExitStack() as room:
            sq = [sb(f"sq{s}", [128, COLS], fp32, room) for s in range(KT)]
        sq_lo = [sb(f"sq_lo{s}", [128, COLS], f32r) for s in range(KT)]
        sq_hi = [sb(f"sq_hi{s}", [128, COLS], f32r) for s in range(KT)]
        x1 = sb("x1", [128, COLS], fp32)
        xt_hi = sb("xt_hi", [128, NT, HID], f32r)
        xt_lo = sb("xt_lo", [128, NT, HID], f32r)
        en = [sb(f"en{s}", [128, 2, NT, GJ], f32r) for s in range(2)]
        with ExitStack() as room:
            y_sb = sb("y_sb", [1, BLOCK], fp32, room)
        bd = [sb(f"bd{s}", [128, 2, NT, EIGHT, GJ], f32r) for s in range(2)]
        z2_part = sb("z2_part", [128, HID], fp32)
        z2_sb = [sb(f"z2_sb{s}", [128, HID], fp32) for s in range(2)]
        b1_sb, b2_sb = sb("b1_sb", [128, H1 // 128], fp32), sb("b2_sb", [128, H2 // 128], fp32)
        top3_sb = sb("top3_sb", [128, H2 // 128], fp32)
        ones_f, ones = sb("ones_f", [128, 1], fp32), sb("ones", [128, 1], f32r)
        with ExitStack() as room:
            g_hi, g_lo = [], []
            for s in range(2):
                g_hi.append(sb(f"g_hi{s}", [128, GJ, TILE], f32r, room))
                g_lo.append(sb(f"g_lo{s}", [128, GJ, TILE], f32r, room))
        with ExitStack() as room:
            r_w1 = sb("r_w1", [128, FIELDS, HID], fp32, room)
            r_pair = sb("r_pair", [128, KT, HID], fp32, room)
            r_swap = sb("r_swap", [128, KT, HID], fp32, room)
            r_rows = sb("r_rows", [FIELDS, HID, 2 * FIELDS], fp32, room)
            r_sel = sb("r_sel", [PARTS, KT, 128], fp32, room)
            r_sum3 = sb("r_sum3", [PARTS, GJ], fp32, room)
            r_diag = sb("r_diag", [128, 2, EIGHT, GJ], fp32, room)
            r_tot = sb("r_tot", [FIELDS, HID], fp32, room)
        with ExitStack() as room:
            t_top1 = sb("t_top1", [128, 2, H1], fp32, room)
            t_top2 = sb("t_top2", [128, H1 // 128, H2], fp32, room)
            t_top1d = sb("t_top1d", [DENSE_ROWS, H1], fp32, room)
            top2_hi = sb("top2_hi", [128, H1 // 128, H2], f32r, room)
            top2_lo = sb("top2_lo", [128, H1 // 128, H2], f32r, room)
            h1_f = [sb("h1_f0", [128, BLOCK], fp32, room)]
            top1_hi = sb("top1_hi", [128, 2, H1], f32r, room)
            top1_lo = sb("top1_lo", [128, 2, H1], f32r, room)
            top1d = sb("top1d", [DENSE_ROWS, H1], f32r, room)
            z1_hi.append(sb("z1_hi1", [128, BLOCK], f32r, room))
            z1_lo.append(sb("z1_lo1", [128, BLOCK], f32r, room))
            h1_f.append(sb("h1_f1", [128, BLOCK], fp32, room))
        z2_raw = [e[:, :, :].rearrange("p f d -> p (f d)")[:, 0:BLOCK].rearrange("p (n h) -> p n h", h=HID) for e in emb]
        y_w, y_hi, y_lo = x1[:, :], xt_hi[:, :, :].rearrange("p n h -> p (n h)"), xt_lo[:, :, :].rearrange("p n h -> p (n h)")
        z1_dram = nc.dram_tensor("z1_dram", [2, 128, BATCH], fp32, kind="Internal").ap()
        z2_dram = nc.dram_tensor("z2_dram", [BATCH, HID], fp32, kind="Internal").ap()

        p_sum = [pb(f"p_sum{s}", [128, COLS]) for s in range(2)]
        p_x1 = pb("p_x1", [128, COLS])
        p_xt = pb("p_xt", [128, NT, HID])
        p_misc = pb("p_misc", [128, 512])
        p_et = (p_misc[:, :].bitcast(bf16), p_xt[:, :, :].rearrange("p n h -> p (n h)").bitcast(bf16))
        p_g = pb("p_g", [128, 2, 512])
        p_z2 = pb("p_z2", [128, 512])

        gather_begun = sem("gather_begun")
        consts_in, top_in, y_out = sem("consts_in"), sem("top_in"), sem("y_out")
        ids_in = [sem(f"ids_in{s}") for s in range(2)]
        emb_in = [sem(f"emb_in{s}") for s in range(2)]
        bd_in = [sem(f"bd_in{s}") for s in range(2)]
        w1_high = sem("w1_high")
        prep = sem("prep")
        parts_a, parts_b = sem("parts_a"), sem("parts_b")
        et_mm = sem("et_mm")
        et_a, et_b = sem("et_a"), sem("et_b")
        en_mm, en_h, en_l = sem("en_mm"), sem("en_h"), sem("en_l")
        sum_mm, sq_done, hi_done, lo_done, prod_mm = (sem(n) for n in ("sum_mm", "sq_done", "hi_done", "lo_done", "prod_mm"))
        x1_out, xt_mm, xt_h, xt_l = sem("x1_out"), sem("xt_mm"), sem("xt_h"), sem("xt_l")
        g_mm, g_h, g_l = sem("g_mm"), sem("g_h"), sem("g_l")
        z2_mm, z2_a, z2_b = sem("z2_mm"), sem("z2_a"), sem("z2_b")
        z1_saved = [sem(f"z1_saved{s}") for s in range(2)]
        z2_saved = [sem(f"z2_saved{s}") for s in range(2)]
        block_in = [sem(f"block_in{s}") for s in range(2)]
        top_hi, top_ready, dense_ready, dense_hi = sem("top_hi"), sem("top_ready"), sem("dense_ready"), sem("dense_hi")
        gate = sem("gate")
        zt_mm, zt_h, zt_l = sem("zt_mm"), sem("zt_h"), sem("zt_l")
        h1_mm, h1_relu, h1_h, h1_l = sem("h1_mm"), sem("h1_relu"), sem("h1_h"), sem("h1_l")
        h2_mm, h2_relu = sem("h2_mm"), sem("h2_relu")
        yw_half, yw, yh, yl = sem("yw_half"), sem("yw"), sem("yh"), sem("yl")
        y_mm, y_copied = sem("y_mm"), sem("y_copied")

        PREPARED = 15
        TOP1_READY, TOP2_READY = 3, 4

        def part(a):
            return parts[:, :, a, :].rearrange("p d f -> p f d")

        def g_view(buf, c, h):
            b = 32 * c + 16 * h
            return buf[:, :, b:b + 16].rearrange("p j (r m) -> p r m j", r=2)

        def g_bank_view():
            return p_g[:, :, 0:EIGHT * GJ].rearrange("p r (m j) -> p r m j", j=GJ)

        def cnt(t, per_tile, more=0):
            reg, at = t
            if reg is None:
                return per_tile * at + more
            return reg * (2 * per_tile) + (per_tile * at + more)

        def pair_cnt(t, per_two, more=0):
            reg, at = t
            if reg is None:
                return per_two * (at // 2) + more
            return reg * per_two + (per_two * (at // 2) + more)

        def row_of(t):
            reg, at = t
            return at * TILE if reg is None else reg * (2 * TILE) + at * TILE

        def highs_by_dve(steps):
            return sum((n % KT) not in HI_ON_ACT for n in range(steps))

        def ge(eng, s, value):
            if not isinstance(value, int) or value > 0:
                eng.wait_ge(s, value)

        def over_tiles(eng, tile):
            tile((None, 0), 0, first=True, last=False)
            with eng.Fori(0, (TILES - 2) // 2) as i:
                tile((i, 1), 1, first=False, last=False)
                tile((i, 2), 0, first=False, last=False)
            tile((None, TILES - 1), 1, first=False, last=True)

        PARTS_AT = (3 * KT - 1, 3 * KT - 1, 3 * KT, 3 * KT)
        ET_AT = (3 * KT + 2, 3 * KT + 3)
        Z2_STEPS = range(KT + 3, STEPS)
        XT_AT, G0_AT, G1_AT = 1, 3, 0

        block = ctx.enter_context(nc.Block())

        @block.sync
        def _(sp):
            def load_ids(t, s, after=None):
                row = row_of(t) if t[0] is None else sp.snap(row_of(t))
                if after is not None:
                    sp.wait_ge(emb_in[s], after)
                sp.dma_start(ids_sb[s][:, :], ids[bass.ds(row, TILE), :]).then_inc(ids_in[s], 16)

            load_ids((None, 0), 0)
            load_ids((None, 1), 1)
            for dst, src in ((r_sel[:, :, :], c_sel), (r_sum3[:, :], c_sum3), (ident[:, :], c_ident),
                             (r_diag[:, :, :, :], c_diag), (r_rows[:, :, :], w0_rows),
                             (r_pair[:, :, :], w0_pair), (r_swap[:, :, :], w0_swap), (r_w1[:, :, :], w1t), (b1_sb[:, :], b1),
                             (b2_sb[:, :], b2), (top3_sb[:, :], top3)):
                sp.dma_start(dst, src).then_inc(consts_in, 16)

            def before(t):
                return t[0], t[1] - 1

            def save_z1(t, s):
                row = row_of(t) if t[0] is None else sp.snap(row_of(t))
                for part, g in ((0, g_hi[s]), (1, g_lo[s])):
                    sp.dma_start(z1_dram[part, :, bass.ds(row, TILE)], g[:, FIELDS, :].bitcast(fp32)).then_inc(z1_saved[s], 16)

            def save_z2(t, s):
                row = row_of(t) if t[0] is None else sp.snap(row_of(t))
                sp.wait_ge(z2_b, cnt(t, 1, 1))
                sp.dma_start(z2_dram[bass.ds(row, TILE), :], z2_sb[s][:, :]).then_inc(z2_saved[s], 16)

            def load_block(n):
                s, cols = n % 2, slice(n * BLOCK, (n + 1) * BLOCK)
                for dst, src in ((z1_hi[s][:, :].bitcast(fp32), z1_dram[0, :, cols]),
                                 (z1_lo[s][:, :].bitcast(fp32), z1_dram[1, :, cols]),
                                 (z2_raw[s], z2_dram[cols, :].rearrange("(t p) h -> p t h", p=TILE)),
                                 (t_dense[s][:, :], dense_t[:, cols])):
                    sp.dma_start(dst, src).then_inc(block_in[s], 16)

            def tile(t, s, more, first=False, last=False):
                for c in range(CHUNKS):
                    cs = c % 2
                    if c == CHUNKS - 1 and last:
                        sp.wait_ge(gate, 1)
                        for dst, src in ((t_top1[:, :, :], top1.rearrange("(k p) n -> p k n", p=128)), (t_top1d[:, :], top1_dense),
                                         (t_top2[:, :, :], top2.rearrange("(k p) n -> p k n", p=128))):
                            sp.dma_start(dst, src).then_inc(top_in, 16)
                        for b in range(2):
                            sp.wait_ge(z1_saved[b], 32 * 2)
                            sp.wait_ge(z2_saved[b], 16 * 2)
                        load_block(0)
                    if c == 1 and more:
                        load_ids((t[0], t[1] + 2), s, pair_cnt(t, 16 * FIELDS, 16 * FIELDS))
                    sp.wait_ge(en_l, cnt(t, CHUNKS, c + 1))
                    for b in range(8):
                        rows = slice(b * DIM, (b + 1) * DIM)
                        sp.dma_start(bd[cs][rows, :, :, b, 0:FIELDS].bitcast(fp32),
                                     en[cs][rows, :, :, 0:FIELDS].bitcast(fp32)).then_inc(bd_in[cs], 16)
                    if c == 1 and not first:
                        save_z1(before(t), 1 - s)
                if not first:
                    save_z2(before(t), 1 - s)

            sp.wait_ge(prep, PREPARED)
            tile((None, 0), 0, more=True, first=True)
            with sp.Fori(0, (TILES - 4) // 2) as i:
                tile((i, 1), 1, more=True)
                tile((i, 2), 0, more=True)
            tile((None, TILES - 3), 1, more=True)
            tile((None, TILES - 2), 0, more=False)
            tile((None, TILES - 1), 1, more=False, last=True)

            sp.wait_ge(z2_mm, TILES - 1)
            sp.wait_ge(z1_saved[0], 32 * TILES // 2)
            sp.wait_ge(z1_saved[1], 32 * TILES // 4)
            for s in range(2):
                sp.wait_ge(z2_saved[s], 16 * TILES // 4)
            load_block(1)
            sp.wait_ge(g_l, 2 * CHUNKS * TILES)
            save_z1((None, TILES - 1), 1)
            sp.wait_ge(h1_mm, 4)
            sp.wait_ge(z1_saved[1], 32 * TILES // 2)
            for s in range(2):
                sp.wait_ge(z2_saved[s], 16 * 6)
            load_block(2)
            save_z2((None, TILES - 1), 1)
            for n in range(BLOCKS):
                if n == 1:
                    sp.wait_ge(h1_mm, 8)
                    for s in range(2):
                        sp.wait_ge(z2_saved[s], 16 * TILES // 2)
                    load_block(3)
                sp.wait_ge(y_copied, n + 1)
                sp.dma_start(out[:, n * BLOCK:(n + 1) * BLOCK], y_sb[:, :]).then_inc(y_out, 16)
            sp.wait_ge(y_out, 16 * BLOCKS)

        @block.gpsimd
        def _(pool):
            def gather(t, s, first):
                if first:
                    pool.wait_ge(ids_in[s], 16)
                else:
                    pool.wait_ge(ids_in[s], t * 16 + 16)
                    pool.wait_ge(parts_b, t * 4 + (2 * s - 3))
                    pool.sem_inc(gather_begun, 1)
                for f in range(FIELDS):
                    nc.gpsimd.indirect_dma_start(
                        out=emb[s][:, f, :], out_offset=None, in_=tables[f],
                        in_offset=bass.IndirectOffsetOnAxis(ap=ids_sb[s][:, f:f + 1], axis=0)).then_inc(emb_in[s], 16)

            gather(0, 0, True)
            gather(0, 1, True)
            with pool.Fori(1, TILES // 2) as pair:
                gather(pair, 0, False)
                gather(pair, 1, False)

        @block.tensor
        def _(pe):
            def embeddings_t(t, r, s):
                pe.wait_ge(parts_b, cnt(t, 2, 2))
                for d in range(8):
                    last = nc.tensor.transpose(p_et[r][0:PARTS, d * 128:(d + 1) * 128],
                                               parts[:, 8 * r + d, :, :].rearrange("p a f -> p (a f)"), ident_b[:, :])
                last.then_inc(et_mm, 1)

            def pair_sums(t, s, step, between=None):
                c, k = divmod(step, KT)
                ge(pe, sq_done, cnt(t, STEPS, step - 1))
                for half in range(2):
                    b = c * 32 + half * 16
                    mm = nc.tensor.matmul(p_sum[step % 2][:, half * COLS // 2:(half + 1) * COLS // 2], sel[:, k, :],
                                          emb_t[s][:, b:b + 16, :].rearrange("p b d -> p (b d)"), start=True, stop=True)
                    if half == 0 and between is not None:
                        between()
                mm.then_inc(sum_mm, 1)

            def products(t, step):
                c, k = divmod(step, KT)
                if k == 0:
                    ge(pe, x1_out, cnt(t, CHUNKS, c))
                pe.wait_ge(lo_done, cnt(t, STEPS, step + 1))
                if k < FULL:
                    nc.tensor.matmul(p_x1[:, :], v_hi[:, k, :], sq_hi[k][:, :], start=(k == 0), stop=False)
                    nc.tensor.matmul(p_x1[:, :], v_lo[:, k, :], sq_hi[k][:, :], start=False, stop=False)
                    nc.tensor.matmul(p_x1[:, :], v_hi[:, k, :], sq_lo[k][:, :], start=False, stop=False).then_inc(prod_mm, 1)
                else:
                    nc.tensor.matmul(p_x1[:, :], v_hi[0:REST_ROWS, k, :], sq_hi[k][0:REST_ROWS, :], start=False,
                                     stop=True).then_inc(prod_mm, 1)

            def embeddings_n(t, s, c):
                ge(pe, en_l, cnt(t, CHUNKS, c))
                if c == 0:
                    pe.wait_ge(et_a, cnt(t, 1, 1))
                for n in range(NT):
                    b = c * 32 + n * 8
                    mm = nc.tensor.matmul(p_misc[:, n * GJ:(n + 1) * GJ],
                                            emb_t[s][:, b:b + 8, :].rearrange("p b d -> p (b d)"), sum3[:, :],
                                            start=True, stop=True)
                mm.then_inc(en_mm, 1)

            def x1_transposed(q):
                pe.wait_ge(x1_out, q)
                ge(pe, xt_l, q - 1)
                for n in range(NT):
                    last = nc.tensor.transpose(p_xt[:, n, :], x1[:, n * 128:(n + 1) * 128], ident[:, :])
                last.then_inc(xt_mm, 1)

            def g_half(q, cs, h):
                if h == 0:
                    pe.wait_ge(xt_l, q)
                    pe.wait_ge(bd_in[cs], bd_count[0])
                ge(pe, g_l, q * 2 - 2 + h)
                for n in (2 * h, 2 * h + 1):
                    o = p_g[:, n % 2, 0:EIGHT * GJ]
                    b_hi = bd[cs][:, 0, n, :, :].rearrange("p b j -> p (b j)")
                    b_lo = bd[cs][:, 1, n, :, :].rearrange("p b j -> p (b j)")
                    nc.tensor.matmul(o, xt_hi[:, n, :], b_hi, start=True, stop=False)
                    nc.tensor.matmul(o, xt_lo[:, n, :], b_hi, start=False, stop=False)
                    last = nc.tensor.matmul(o, xt_hi[:, n, :], b_lo, start=False, stop=True)
                last.then_inc(g_mm, 1)

            bd_count = [None]

            def z2_high(s, j):
                nc.tensor.matmul(p_z2[:, 0:2 * HID], g_hi[s][:, j, :], w1[:, j, :], start=(j == 0), stop=False)

            def z2_low(s, j, gated=False):
                mm = nc.tensor.matmul(p_z2[:, 0:HID], g_lo[s][:, j, :], w1[:, j, 0:HID], start=False,
                                      stop=(j == FIELDS - 1))
                if j == FIELDS - 1:
                    mm.then_inc(z2_mm, 1)
                if gated and j == GATE - 1:
                    mm.then_inc(gate, 1)

            def tile(t, s, first, last):
                for step in range(STEPS):
                    c, k = divmod(step, KT)
                    fields = []
                    if not first and step in Z2_STEPS:
                        n = step - Z2_STEPS[0]
                        if n == 0:
                            pe.wait_ge(g_l, cnt(t, 2 * CHUNKS))
                            ge(pe, z2_b, cnt(t, 1, -1))
                        fields = list(range(FIELDS * n // len(Z2_STEPS), FIELDS * (n + 1) // len(Z2_STEPS)))
                    for j in fields:
                        z2_high(1 - s, j)
                    for j in fields[:-1]:
                        z2_low(1 - s, j, last)
                    if k == 0:
                        embeddings_n(t, s, c)
                    between = (lambda: z2_low(1 - s, fields[-1], last)) if fields else None
                    if step + AHEAD < STEPS:
                        pair_sums(t, s, step + AHEAD, between)
                    elif not last:
                        if step + AHEAD == STEPS:
                            pe.wait_ge(et_a, cnt(t, 1, 2))
                            pe.wait_ge(et_b, cnt(t, 1, 2))
                        pair_sums((t[0], t[1] + 1), 1 - s, step + AHEAD - STEPS, between)
                    elif fields:
                        between()
                    if step == ET_AT[1] and not last:
                        pe.wait_ge(xt_l, cnt(t, CHUNKS, c))
                        embeddings_t((t[0], t[1] + 1), 1, 1 - s)
                    if k == G1_AT and not (first and c < 2):
                        g_half(cnt(t, CHUNKS, c - 1), c % 2, 1)
                    products(t, step)
                    if not (first and c == 0):
                        q = cnt(t, CHUNKS, c)
                        ps = (c - 1) % 2
                        bd_count[0] = cnt(t, 2 * 128, 128 * ((c + 1) // 2))
                        if k == XT_AT:
                            x1_transposed(q)
                        if k == G0_AT:
                            g_half(q, ps, 0)
                    if step == ET_AT[0] and not last:
                        pe.wait_ge(en_l, cnt(t, CHUNKS, c + 1))
                        embeddings_t((t[0], t[1] + 1), 0, 1 - s)

            pe.wait_ge(prep, PREPARED)
            embeddings_t((None, 0), 0, 0)
            embeddings_t((None, 0), 1, 0)
            pe.wait_ge(et_a, 1)
            pe.wait_ge(et_b, 1)
            for step in range(AHEAD):
                pair_sums((None, 0), 0, step)
            over_tiles(pe, tile)

            q = TILES * CHUNKS
            h1_banks = [p_sum[0][:, :], p_sum[1][:, :], p_misc[:, :], p_xt[:, :, :].rearrange("p n h -> p (n h)")]

            def z2_transposed(n):
                pe.wait_ge(block_in[n % 2], 64 * (n // 2 + 1))
                ge(pe, zt_l, n)
                for i in range(NT):
                    last = nc.tensor.transpose(p_x1[:, i * HID:(i + 1) * HID], z2_raw[n % 2][:, i, :], ident[:, :])
                last.then_inc(zt_mm, 1)

            def layer1(n, m, halves=(0, 1)):
                s = n % 2
                ms = slice(m * 128, (m + 1) * 128)
                o = h1_banks[m]
                if 0 in halves:
                    ge(pe, h1_h, 4 * (n - 1) + m + 1)
                    nc.tensor.matmul(o, top1d[:, ms], dense[s][:, :], start=True, stop=False)
                for k in halves:
                    z_hi, z_lo = ((z1_hi[s], z1_lo[s]), (z2_hi, z2_lo))[k]
                    if k == 1:
                        pe.wait_ge(zt_l, n + 1)
                    nc.tensor.matmul(o, top1_hi[:, k, ms], z_hi[:, :], start=False, stop=False)
                    nc.tensor.matmul(o, top1_lo[:, k, ms], z_hi[:, :], start=False, stop=False)
                    last = nc.tensor.matmul(o, top1_hi[:, k, ms], z_lo[:, :], start=False, stop=(k == 1))
                if 1 in halves:
                    last.then_inc(h1_mm, 1)

            def layer2(n):
                for m in range(H2 // 128):
                    ms = slice(m * 128, (m + 1) * 128)
                    ge(pe, h2_relu, 2 * (n - 1) + m + 1)
                    for k in range(H1 // 128):
                        pe.wait_ge(h1_l, 4 * n + k + 1)
                        nc.tensor.matmul(p_g[:, m, :], top2_hi[:, k, ms], h1_hi[:, k, :], start=(k == 0), stop=False)
                        nc.tensor.matmul(p_g[:, m, :], top2_lo[:, k, ms], h1_hi[:, k, :], start=False, stop=False)
                        last = nc.tensor.matmul(p_g[:, m, :], top2_hi[:, k, ms], h1_lo[:, k, :], start=False,
                                                stop=(k == H1 // 128 - 1))
                    last.then_inc(h2_mm, 1)

            def layer3(n):
                ge(pe, y_copied, n)
                if n < BLOCKS - 1:
                    pe.wait_ge(yl, n + 1)
                    nc.tensor.matmul(p_z2[0:1, :], ones[:, :], y_hi, start=True, stop=False)
                    last = nc.tensor.matmul(p_z2[0:1, :], ones[:, :], y_lo, start=False, stop=True)
                else:
                    for k in range(H2 // 128):
                        pe.wait_ge(h2_relu, 2 * n + k + 1)
                        last = nc.tensor.matmul(p_z2[0:1, :], top3_sb[:, k:k + 1], h2_f[:, k, :], start=(k == 0),
                                                stop=(k == H2 // 128 - 1))
                last.then_inc(y_mm, 1)

            bd_count[0] = 2 * 128 * TILES
            g_half(q - 1, 0, 1)
            x1_transposed(q)
            z2_transposed(0)
            pe.wait_ge(top_ready, TOP1_READY)
            pe.wait_ge(dense_ready, 1)
            layer1(0, 0, (0,))
            g_half(q, 1, 0)
            layer1(0, 0, (1,))
            layer1(0, 1, (0,))
            g_half(q, 1, 1)
            layer1(0, 1, (1,))
            pe.wait_ge(en_l, q)
            layer1(0, 2)
            layer1(0, 3)
            z2_transposed(1)
            pe.wait_ge(g_l, 2 * q)
            pe.wait_ge(z2_b, TILES - 1)
            for j in range(FIELDS):
                z2_high(1, j)
                z2_low(1, j)
            pe.wait_ge(top_ready, TOP2_READY)
            layer2(0)
            pe.wait_ge(z2_b, TILES)
            for n in range(1, BLOCKS):
                pe.wait_ge(dense_ready, n + 1)
                for m in range(H1 // 128):
                    layer1(n, m)
                if n + 1 < BLOCKS:
                    z2_transposed(n + 1)
                layer3(n - 1)
                layer2(n)
            layer3(BLOCKS - 1)

        @block.scalar
        def _(act):
            def square(t, step):
                k = step % KT
                act.wait_ge(sum_mm, cnt(t, STEPS, step + 1))
                ge(act, prod_mm, cnt(t, STEPS, step - KT + 1))
                rows = 128 if k < FULL else REST_ROWS
                if k in HI_ON_ACT:
                    nc.scalar.activation(sq_hi[k][0:rows, :], p_sum[step % 2][0:rows, :], ACT.Square)
                nc.scalar.activation(sq[k][0:rows, :], p_sum[step % 2][0:rows, :], ACT.Square).then_inc(sq_done, 1)

            def split(t, s, n):
                if n == 0:
                    act.wait_ge(emb_in[s], pair_cnt(t, 16 * FIELDS, 16 * FIELDS))
                    ge(act, et_mm, cnt(t, 2))
                    nc.scalar.copy(part(0), emb[s][:, :, :]).then_inc(parts_a, 1)
                if n == 2:
                    act.wait_ge(parts_b, cnt(t, 2, 1))
                    nc.scalar.copy(part(1), resid[:, :, :]).then_inc(parts_a, 1)

            def transposed_a(t, s):
                act.wait_ge(et_mm, cnt(t, 2, 1))
                nc.scalar.copy(emb_t[s][:, :, 0:8].rearrange("p b d -> p d b"),
                               p_et[0][0:PARTS, :].rearrange("p (d b) -> p d b", b=TILE)).then_inc(et_a, 1)

            def x1_leaves(q):
                act.wait_ge(prod_mm, q * KT)
                ge(act, xt_mm, q - 1)
                nc.scalar.copy(x1[:, :], p_x1[:, :]).then_inc(x1_out, 1)

            def g_out(t_g, q, s, c, h):
                act.wait_ge(g_mm, q * 2 - 1 + h)
                if c == 0 and h == 0:
                    ge(act, z2_mm, cnt(t_g, 1, -1))
                    if t_g[0] is not None or t_g[1] > 1:
                        act.wait_ge(z1_saved[s], pair_cnt(t_g, 32))
                nc.scalar.copy(g_view(g_hi[s], c, h), g_bank_view()).then_inc(g_h, 1)

            def tile(t, s, first, last):
                for step in range(STEPS):
                    c, k = divmod(step, KT)
                    before = not (first and c == 0)
                    q = cnt(t, CHUNKS, c)
                    pt = s if c > 0 else 1 - s
                    if k == 0 and before:
                        x1_leaves(q)
                    if k == G1_AT + 1 and not (first and c < 2):
                        g_out(t, cnt(t, CHUNKS, c - 1), s if c > 1 else 1 - s, (c - 2) % CHUNKS, 1)
                    if k == 1:
                        act.wait_ge(en_mm, cnt(t, CHUNKS, c + 1))
                        if not (first and c < 2):
                            act.wait_ge(bd_in[c % 2], cnt(t, 2 * 128, 128 * (c // 2)))
                        nc.scalar.copy(en[c % 2][:, 0, :, :], p_misc[:, 0:NT * GJ].rearrange("p (n j) -> p n j", j=GJ)).then_inc(en_h, 1)
                    if k == XT_AT + 1 and before:
                        act.wait_ge(xt_mm, q)
                        ge(act, g_mm, q * 2 - 2)
                        nc.scalar.copy(xt_hi[:, :, :], p_xt[:, :, :]).then_inc(xt_h, 1)
                    if k == G0_AT + 1 and before:
                        g_out(t, q, pt, (c - 1) % CHUNKS, 0)
                    if step == ET_AT[0] + 1 and not last:
                        transposed_a((t[0], t[1] + 1), 1 - s)
                    if step + AHEAD < STEPS:
                        square(t, step + AHEAD)
                    elif not last:
                        square((t[0], t[1] + 1), step + AHEAD - STEPS)
                    for n in (0, 2):
                        if step == PARTS_AT[n] and not last:
                            split((t[0], t[1] + 1), 1 - s, n)
                    if step == STEPS - AHEAD and last:
                        act.wait_ge(top_in, 16 * 3)
                        nc.scalar.copy(top1_hi[:, :, :], t_top1[:, :, :]).then_inc(top_hi, 1)
                    if step == STEPS - 1 and not first:
                        act.wait_ge(z2_mm, cnt(t, 1))
                        ge(act, z2_b, cnt(t, 1, -1))
                        nc.scalar.copy(z2_part[:, :], p_z2[:, HID:2 * HID]).then_inc(z2_a, 1)

            act.wait_ge(consts_in, 16 * 11)
            nc.scalar.copy(w1[:, :, 0:HID], r_w1[:, :, :]).then_inc(w1_high, 1)
            split((None, 0), 0, 0)
            split((None, 0), 0, 2)
            transposed_a((None, 0), 0)
            for step in range(AHEAD):
                square((None, 0), step)
            over_tiles(act, tile)

            q = TILES * CHUNKS
            h1_banks = [p_sum[0][:, :], p_sum[1][:, :], p_misc[:, :], p_xt[:, :, :].rearrange("p n h -> p (n h)")]

            def z2_parts(n):
                act.wait_ge(zt_mm, n + 1)
                ge(act, h1_mm, 4 * n)
                nc.scalar.copy(z2_hi[:, :], p_x1[:, :]).then_inc(zt_h, 1)

            def layer1_out(n, m):
                act.wait_ge(h1_mm, 4 * n + m + 1)
                ge(act, h2_mm, 2 * n)
                ge(act, h1_l, 4 * n + m - 1)
                nc.scalar.activation(h1_f[m % 2][:, :], h1_banks[m], ACT.Relu, bias=b1_sb[:, m:m + 1]).then_inc(h1_relu, 1)
                nc.scalar.activation(h1_hi[:, m, :], h1_banks[m], ACT.Relu, bias=b1_sb[:, m:m + 1]).then_inc(h1_h, 1)

            def layer2_out(n):
                for m in range(H2 // 128):
                    act.wait_ge(h2_mm, 2 * n + m + 1)
                    ge(act, y_mm, n)
                    nc.scalar.activation(h2_f[:, m, :], p_g[:, m, :], ACT.Relu, bias=b2_sb[:, m:m + 1]).then_inc(h2_relu, 1)

            def weighted_high(n):
                act.wait_ge(yw, n + 1)
                ge(act, y_mm, n)
                nc.scalar.copy(y_hi, y_w).then_inc(yh, 1)

            def layer3_out(n):
                act.wait_ge(y_mm, n + 1)
                ge(act, y_out, 16 * n)
                nc.scalar.copy(y_sb[:, :], p_z2[0:1, :]).then_inc(y_copied, 1)

            x1_leaves(q)
            g_out((None, TILES - 1), q - 1, 1, 2, 1)
            act.wait_ge(xt_mm, q)
            act.wait_ge(g_mm, q * 2 - 2)
            nc.scalar.copy(xt_hi[:, :, :], p_xt[:, :, :]).then_inc(xt_h, 1)
            z2_parts(0)
            g_out((None, TILES - 1), q, 1, 3, 0)
            layer1_out(0, 0)
            g_out((None, TILES - 1), q, 1, 3, 1)
            layer1_out(0, 1)
            layer1_out(0, 2)
            layer1_out(0, 3)
            z2_parts(1)
            nc.scalar.copy(top2_hi[:, :, :], t_top2[:, :, :]).then_inc(top_hi, 1)
            act.wait_ge(z2_mm, TILES)
            act.wait_ge(z2_b, TILES - 1)
            nc.scalar.copy(z2_part[:, :], p_z2[:, HID:2 * HID]).then_inc(z2_a, 1)
            layer2_out(0)
            for n in range(1, BLOCKS):
                for m in range(H1 // 128):
                    layer1_out(n, m)
                    if m == 0:
                        weighted_high(n - 1)
                if n + 1 < BLOCKS:
                    z2_parts(n + 1)
                layer3_out(n - 1)
                layer2_out(n)
            layer3_out(BLOCKS - 1)

        @block.vector
        def _(dve):
            done = [0]

            def chained(ins):
                ins.then_inc(prep, 1)
                done[0] += 1
                dve.wait_ge(prep, done[0])

            dve.wait_ge(consts_in, 16 * 11)
            nc.vector.tensor_copy(sel[:, :, :], r_sel[:, :, :]).then_inc(prep, 1)
            nc.vector.tensor_copy(sum3[:, :], r_sum3[:, :]).then_inc(prep, 1)
            nc.vector.memset(ones_f[:, :], 1.0).then_inc(prep, 1)
            nc.vector.tensor_copy(ident_b[:, :], ident[:, :]).then_inc(prep, 1)
            for s in range(2):
                nc.vector.tensor_copy(bd[s][:, :, :, :, :],
                                      r_diag[:, :, None, :, :].broadcast_to([128, 2, NT, EIGHT, GJ])
                                      ).then_inc(prep, 1)
            done[0] = 6
            dve.wait_ge(prep, done[0])
            chained(nc.vector.tensor_copy(ones[:, :], ones_f[:, :]))
            chained(nc.vector.tensor_tensor(r_pair[:, :, :], r_pair[:, :, :], r_swap[:, :, :], ALU.add))
            chained(nc.vector.tensor_reduce(r_tot[:, :], r_rows[:, :, :], AX.X, ALU.add))
            chained(nc.vector.tensor_scalar(r_tot[:, :], r_tot[:, :], -0.5, None, ALU.mult))
            chained(nc.vector.tensor_scalar(r_swap[:, :, :], r_pair[:, :, :], 0.5, None, ALU.mult))
            chained(nc.vector.tensor_tensor(r_swap[0:FIELDS, 0, :], r_pair[0:FIELDS, 0, :], r_tot[:, :], ALU.add))
            chained(nc.vector.tensor_copy(v_hi[:, :, :], r_swap[:, :, :]))
            nc.vector.tensor_tensor(v_lo[:, :, :], r_swap[:, :, :], v_hi[:, :, :], ALU.subtract).then_inc(prep, 1)
            done[0] += 1
            dve.wait_ge(prep, done[0])
            rest = slice(64, REST_ROWS)
            nc.vector.tensor_tensor(v_hi[rest, FULL, :], r_swap[rest, FULL, :], v_hi[rest, FULL, :], ALU.subtract)
            dve.wait_ge(w1_high, 1)
            nc.vector.tensor_tensor(w1[:, :, HID:2 * HID], r_w1[:, :, :], w1[:, :, 0:HID], ALU.subtract).then_inc(prep, 1)
            assert done[0] + 1 == PREPARED

            def split_rest(t, s, n):
                dve.wait_ge(parts_a, cnt(t, 2, n // 2 + 1))
                if n == 1:
                    nc.vector.tensor_tensor(resid[:, :, :], emb[s][:, :, :], part(0), ALU.subtract).then_inc(parts_b, 1)
                if n == 3:
                    nc.vector.tensor_tensor(part(2), resid[:, :, :], part(1), ALU.subtract).then_inc(parts_b, 1)

            def high(t, step):
                k = step % KT
                rows = 128 if k < FULL else REST_ROWS
                if k not in HI_ON_ACT:
                    dve.wait_ge(sq_done, cnt(t, STEPS, step + 1))
                    nc.vector.tensor_copy(sq_hi[k][0:rows, :], sq[k][0:rows, :]).then_inc(hi_done, 1)

            def low(t, step):
                k = step % KT
                if k in HI_ON_ACT:
                    dve.wait_ge(sq_done, cnt(t, STEPS, step + 1))
                else:
                    dve.wait_ge(hi_done, cnt(t, highs_by_dve(STEPS), highs_by_dve(step + 1)))
                if k < FULL:
                    nc.vector.tensor_tensor(sq_lo[k][:, :], sq[k][:, :], sq_hi[k][:, :], ALU.subtract).then_inc(lo_done, 1)
                else:
                    mid = slice(32, 64)
                    nc.vector.tensor_tensor(sq_hi[k][mid, :], sq[k][mid, :], sq_hi[k][mid, :], ALU.subtract).then_inc(lo_done, 1)

            def g_low(n, s, c, h):
                dve.wait_ge(g_h, n)
                nc.vector.tensor_tensor(g_view(g_lo[s], c, h), g_bank_view(), g_view(g_hi[s], c, h),
                                        ALU.subtract).then_inc(g_l, 1)

            def xt_low(q):
                dve.wait_ge(xt_h, q)
                nc.vector.tensor_tensor(xt_lo[:, :, :], p_xt[:, :, :], xt_hi[:, :, :], ALU.subtract).then_inc(xt_l, 1)

            def transposed_b(t, s):
                dve.wait_ge(et_mm, cnt(t, 2, 2))
                nc.vector.tensor_copy(emb_t[s][:, :, 8:16].rearrange("p b d -> p d b"),
                                      p_et[1][0:PARTS, :].rearrange("p (d b) -> p d b", b=TILE)).then_inc(et_b, 1)

            def z2_of(t, s):
                dve.wait_ge(z2_a, cnt(t, 1, 1))
                if t[0] is not None or t[1] > 1:
                    ge(dve, z2_saved[s], pair_cnt(t, 16))
                nc.vector.tensor_tensor(z2_sb[s][:, :], p_z2[:, 0:HID], z2_part[:, :], ALU.add).then_inc(z2_b, 1)

            def dense_high(n):
                dve.wait_ge(block_in[n % 2], 64 * (n // 2 + 1))
                nc.vector.tensor_copy(dense[n % 2][:, :], t_dense[n % 2][:, :]).then_inc(dense_hi, 1)

            def dense_low(n):
                s, low_rows = n % 2, slice(32, 64)
                dve.wait_ge(dense_hi, n + 1)
                nc.vector.tensor_tensor(dense[s][low_rows, :], t_dense[s][low_rows, :], dense[s][low_rows, :],
                                        ALU.subtract).then_inc(dense_ready, 1)

            def top_step(n):
                low_rows = slice(64, DENSE_ROWS)
                if n == 0:
                    dve.wait_ge(top_in, 16 * 3)
                    nc.vector.tensor_copy(top1d[:, :], t_top1d[:, :]).then_inc(top_ready, 1)
                    dve.wait_ge(prod_mm, (TILES - 1) * STEPS + 3 * KT + 3)
                    dense_high(0)
                if n == 1:
                    dve.wait_ge(top_ready, 1)
                    nc.vector.tensor_tensor(top1d[low_rows, :], t_top1d[low_rows, :], top1d[low_rows, :],
                                            ALU.subtract).then_inc(top_ready, 1)
                    dense_low(0)
                if n == 2:
                    dve.wait_ge(top_hi, 1)
                    nc.vector.tensor_tensor(top1_lo[:, :, :], t_top1[:, :, :], top1_hi[:, :, :], ALU.subtract).then_inc(top_ready, 1)

            def tile(t, s, first, last):
                for step in range(STEPS):
                    c, k = divmod(step, KT)
                    before = not (first and c == 0)
                    q = cnt(t, CHUNKS, c)
                    if k == G1_AT + 1 and not (first and c < 2):
                        g_low(cnt(t, 2 * CHUNKS, 2 * (c - 1)), s if c > 1 else 1 - s, (c - 2) % CHUNKS, 1)
                    if k == 1:
                        dve.wait_ge(en_h, cnt(t, CHUNKS, c + 1))
                        nc.vector.tensor_tensor(en[c % 2][:, 1, :, :], p_misc[:, 0:NT * GJ].rearrange("p (n j) -> p n j", j=GJ),
                                                en[c % 2][:, 0, :, :], ALU.subtract).then_inc(en_l, 1)
                    if k == XT_AT + 1 and before:
                        xt_low(q)
                    if k == G0_AT + 1 and before:
                        g_low(cnt(t, 2 * CHUNKS, 2 * c - 1), s if c > 0 else 1 - s, (c - 1) % CHUNKS, 0)
                    if step == ET_AT[1] and not last:
                        transposed_b((t[0], t[1] + 1), 1 - s)
                    if step + AHEAD < STEPS:
                        high(t, step + AHEAD)
                        low(t, step + AHEAD)
                    elif not last:
                        high((t[0], t[1] + 1), step + AHEAD - STEPS)
                        low((t[0], t[1] + 1), step + AHEAD - STEPS)
                    for n in (1, 3):
                        if step == PARTS_AT[n] and not last:
                            split_rest((t[0], t[1] + 1), 1 - s, n)
                    if last:
                        top_step(step - (STEPS - AHEAD))
                    if step == STEPS - 1 and not first:
                        z2_of((t[0], t[1] - 1), 1 - s)

            split_rest((None, 0), 0, 1)
            split_rest((None, 0), 0, 3)
            transposed_b((None, 0), 0)
            for step in range(AHEAD):
                high((None, 0), step)
                low((None, 0), step)
            over_tiles(dve, tile)
            q = TILES * CHUNKS

            def z2_parts(n):
                dve.wait_ge(zt_h, n + 1)
                nc.vector.tensor_tensor(z2_lo[:, :], p_x1[:, :], z2_hi[:, :], ALU.subtract).then_inc(zt_l, 1)

            def layer1_low(n, m):
                dve.wait_ge(h1_relu, 4 * n + m + 1)
                dve.wait_ge(h1_h, 4 * n + m + 1)
                nc.vector.tensor_tensor(h1_lo[:, m, :], h1_f[m % 2][:, :], h1_hi[:, m, :], ALU.subtract).then_inc(h1_l, 1)

            def weighted(n):
                dve.wait_ge(h2_relu, 2 * n + 2)
                ge(dve, yl, n)
                nc.vector.tensor_scalar(y_w, h2_f[:, 0, :], top3_sb[:, 0:1], None, ALU.mult).then_inc(yw_half, 1)
                dve.wait_ge(yw_half, n + 1)
                nc.vector.scalar_tensor_tensor(y_w, h2_f[:, 1, :], top3_sb[:, 1:2], y_w, ALU.mult, ALU.add).then_inc(yw, 1)

            def weighted_low(n):
                dve.wait_ge(yh, n + 1)
                nc.vector.tensor_tensor(y_lo, y_w, y_hi, ALU.subtract).then_inc(yl, 1)

            g_low(2 * q - 2, 1, 2, 1)
            xt_low(q)
            dve.wait_ge(prod_mm, q * KT)
            z2_parts(0)
            g_low(2 * q - 1, 1, 3, 0)
            layer1_low(0, 0)
            g_low(2 * q, 1, 3, 1)
            layer1_low(0, 1)
            layer1_low(0, 2)
            layer1_low(0, 3)
            dense_high(1)
            dense_low(1)
            z2_parts(1)
            dve.wait_ge(top_hi, 2)
            nc.vector.tensor_tensor(top2_lo[:, :, :], t_top2[:, :, :], top2_hi[:, :, :], ALU.subtract).then_inc(top_ready, 1)
            z2_of((None, TILES - 1), 1)
            for n in range(1, BLOCKS):
                weighted(n - 1)
                for m in range(H1 // 128):
                    layer1_low(n, m)
                    if m == 0:
                        weighted_low(n - 1)
                if n + 1 < BLOCKS:
                    dense_high(n + 1)
                    dense_low(n + 1)
                    z2_parts(n + 1)


def kernel(**inputs):
    import numpy as np
    import concourse.bacc as bacc
    from concourse.bass_utils import run_bass_kernel_spmd

    pairs = [(i, i) for i in range(FIELDS)] + [(i, j) for i in range(FIELDS) for j in range(i + 1, FIELDS)]
    slots = [(n // 128, n % 128, n) for n in range(128 * FULL)]
    slots += [(FULL, at + n, 128 * FULL + n) for at in (0, 32, 64) for n in range(REST)]
    w0 = np.asarray(inputs["L0_rec_W0"]).reshape(HID, FIELDS, FIELDS)
    w0_pair = np.zeros((128, KT, HID), np.float32)
    w0_swap = np.zeros((128, KT, HID), np.float32)
    c_sel = np.zeros((PARTS, KT, 128), np.float32)
    for k, row, n in slots:
        i, j = pairs[n]
        w0_pair[row, k] = w0[:, i, j]
        w0_swap[row, k] = w0[:, j, i]
        for part in range(3):
            c_sel[part * FIELDS + i, k, row] = 1.0
            c_sel[part * FIELDS + j, k, row] = 1.0
    w0_rows = np.concatenate([w0.transpose(1, 0, 2), w0.transpose(2, 0, 1)], axis=2)
    c_sum3 = np.zeros((PARTS, GJ), np.float32)
    for n in range(PARTS):
        c_sum3[n, n % FIELDS] = 1.0
    c_diag = np.zeros((128, 2, EIGHT, GJ), np.float32)
    for p in range(128):
        c_diag[p, 0, p // DIM, FIELDS] = 1.0
    top1 = np.asarray(inputs["W_top1"])
    top1_dense = np.zeros((DENSE_ROWS, H1), np.float32)
    dense_t = np.zeros((DENSE_ROWS, BATCH), np.float32)
    for at in (0, 32, 64):
        top1_dense[at:at + DIM] = top1[2 * HID:]
        dense_t[at:at + DIM] = np.asarray(inputs["dense_ctx"]).T

    arrays = {
        "ids": inputs["ids"], "w0_pair": w0_pair, "w0_swap": w0_swap, "w0_rows": w0_rows,
        "w1t": np.asarray(inputs["L0_rec_W1"]).reshape(HID, HID, FIELDS).transpose(1, 2, 0),
        "top1": top1[:2 * HID], "top1_dense": top1_dense, "b1": np.asarray(inputs["b_top1"]).reshape(H1 // 128, 128).T,
        "top2": inputs["W_top2"], "b2": np.asarray(inputs["b_top2"]).reshape(H2 // 128, 128).T,
        "top3": np.asarray(inputs["W_top3"]).reshape(H2 // 128, 128).T,
        "dense_t": dense_t,
        "c_sel": c_sel, "c_sum3": c_sum3, "c_ident": np.eye(128, dtype=np.float32), "c_diag": c_diag,
    }
    for f in range(FIELDS):
        arrays[f"tbl_{f}"] = inputs[f"tbl_{f}"]
    nc = bacc.Bacc("TRN2", target_bir_lowering=False, num_devices=1)
    feed, ap = {}, {}
    for name, a in arrays.items():
        a = np.ascontiguousarray(a)
        feed[f"in_{name}"] = a
        ap[name] = nc.dram_tensor(f"in_{name}", a.shape, mybir.dt.from_np(a.dtype), kind="ExternalInput").ap()
    out = nc.dram_tensor("out_y", (1, BATCH), mybir.dt.float32, kind="ExternalOutput").ap()
    tables = [ap.pop(f"tbl_{f}") for f in range(FIELDS)]
    cin_tower_kernel(nc, tables=tables, out=out, **ap)
    r = run_bass_kernel_spmd(nc, [feed], core_ids=[0])
    return r.results[0]["out_y"].reshape(BATCH, 1)
```
